# Optimizing a Trainium2 kernel written in Bass

```python
import numpy as np
import jax
import jax.numpy as jnp

def _softmax(x, axis=-1):
    return jax.nn.softmax(x, axis=axis)

def _gelu(x):
    return jax.nn.gelu(x, approximate=True)

def _silu(x):
    return jax.nn.silu(x)

def _sigmoid(x):
    return jax.nn.sigmoid(x)

def _layernorm(x, axis=-1, eps=1e-05):
    m = jnp.mean(x, axis=axis, keepdims=True)
    v = jnp.var(x, axis=axis, keepdims=True)
    return (x - m) / jnp.sqrt(v + eps)

def _scatter_add(tgt, idx, src, axis=0):
    return tgt.at[idx].add(src)

def _segment_sum(src, seg, n):
    return jax.ops.segment_sum(src, seg, n)
kernel_name = 'mk_flamingo_gated_d1_seqx_r4_651730'

def setup_inputs(seed: int=0):
    np.random.seed(seed)
    _w = jnp.asarray

    def _rec_inputs():
        import jax
        import jax.numpy as jnp
        _rk = jax.random.key(seed)
        x = 7.22e-05 + 1 * jax.random.normal(jax.random.fold_in(_rk, 1), (32, 128, 256), jnp.float32)
        _lenS = 128 - jax.random.randint(jax.random.fold_in(_rk, 7), (32,), 0, max(1, 128 // 4) + 1, jnp.int32)
        _lenS2 = 128 - jax.random.randint(jax.random.fold_in(_rk, 8), (32,), 0, max(1, 128 // 4) + 1, jnp.int32)
        _ctx_1024P = jax.random.normal(jax.random.fold_in(_rk, 11), (32, 16, 256), jnp.float32)
        _ctx_1024c = jax.random.dirichlet(jax.random.fold_in(_rk, 511), 0.3 * jnp.ones((16,), jnp.float32), (32, 128))
        _ctx_1024t = jnp.einsum('bsk,bkd->bsd', _ctx_1024c, _ctx_1024P)
        _ctx_1024t = _ctx_1024t * jax.lax.rsqrt(jnp.mean(jnp.square(_ctx_1024t)) + 1e-12) * 0.953939
        ctx_1024 = 4.13588e-05 + 0.999923 * (_ctx_1024t + 0.3 * jax.random.normal(jax.random.fold_in(_rk, 611), (32, 128, 256), jnp.float32))
        _g = jax.random.normal(jax.random.fold_in(_rk, 9001), (2, 1), jnp.float32)
        _g = jnp.sign(_g) * jnp.maximum(jnp.abs(_g), 1.0) + (_g == 0) * 1.0
        g_xattn = _g[0]
        g_ffn = _g[1]
        return (x, ctx_1024, g_xattn, g_ffn)
    x, ctx_1024, g_xattn, g_ffn = _rec_inputs()

    def _L0_xattn_setup():
        import jax, jax.numpy as jnp
        import numpy as np
        B, S, D, H = (4, 512, 256, 16)
        DEPTH = D // H
        NEG = -1000000000.0

        def _split_heads(x):
            b, s, _ = x.shape
            return x.reshape(b, s, H, DEPTH).transpose(0, 2, 1, 3)
        key = jax.random.key(seed)
        ks = jax.random.split(key, 11)
        scale = 1.0 / np.sqrt(D)
        return {'q': jax.random.normal(ks[0], (B, S, D), jnp.float32), 'k': jax.random.normal(ks[1], (B, S, D), jnp.float32), 'v': jax.random.normal(ks[2], (B, S, D), jnp.float32), 'wq_w': jax.random.normal(ks[3], (D, D), jnp.float32) * scale, 'wq_b': jax.random.normal(ks[4], (D,), jnp.float32) * 0.01, 'wk_w': jax.random.normal(ks[5], (D, D), jnp.float32) * scale, 'wk_b': jax.random.normal(ks[6], (D,), jnp.float32) * 0.01, 'wv_w': jax.random.normal(ks[7], (D, D), jnp.float32) * scale, 'wv_b': jax.random.normal(ks[8], (D,), jnp.float32) * 0.01, 'dense_w': jax.random.normal(ks[9], (D, D), jnp.float32) * scale, 'dense_b': jax.random.normal(ks[10], (D,), jnp.float32) * 0.01}
    _L0_xattn_all = _L0_xattn_setup()
    _L0_xattn_in = {k: v for k, v in _L0_xattn_all.items() if k in ('wq_w', 'wq_b', 'wk_w', 'wk_b', 'wv_w', 'wv_b', 'dense_w', 'dense_b')}
    del _L0_xattn_all

    def _L0_ffn_setup():
        import jax, jax.numpy as jnp
        import numpy as np
        B, S, D, E, F = (2, 512, 256, 14, 512)
        key = jax.random.key(seed)
        k = jax.random.split(key, 4)
        h = jax.random.normal(k[0], (B, S, D), dtype=jnp.float32)
        router_w = jax.random.normal(k[1], (D, E), dtype=jnp.float32) * 0.02
        w1 = jax.random.uniform(k[2], (E, D, F), dtype=jnp.float32, minval=-1.0, maxval=1.0) * float(np.sqrt(6.0 / D))
        w2 = jax.random.uniform(k[3], (E, F, D), dtype=jnp.float32, minval=-1.0, maxval=1.0) * float(np.sqrt(6.0 / F))
        b1 = jnp.zeros((E, F), dtype=jnp.float32)
        b2 = jnp.zeros((E, D), dtype=jnp.float32)
        return {'h': h, 'router_w': router_w, 'w1': w1, 'b1': b1, 'w2': w2, 'b2': b2}
    _L0_ffn_all = _L0_ffn_setup()
    _L0_ffn_in = {k: v for k, v in _L0_ffn_all.items() if k in ('router_w', 'w1', 'b1', 'w2', 'b2')}
    del _L0_ffn_all
    return {'x': x, 'ctx_1024': ctx_1024, 'g_xattn': g_xattn, 'g_ffn': g_ffn, 'L0_xattn_wq_w': _L0_xattn_in['wq_w'], 'L0_xattn_wq_b': _L0_xattn_in['wq_b'], 'L0_xattn_wk_w': _L0_xattn_in['wk_w'], 'L0_xattn_wk_b': _L0_xattn_in['wk_b'], 'L0_xattn_wv_w': _L0_xattn_in['wv_w'], 'L0_xattn_wv_b': _L0_xattn_in['wv_b'], 'L0_xattn_dense_w': _L0_xattn_in['dense_w'], 'L0_xattn_dense_b': _L0_xattn_in['dense_b'], 'L0_ffn_router_w': _L0_ffn_in['router_w'], 'L0_ffn_w1': _L0_ffn_in['w1'], 'L0_ffn_b1': _L0_ffn_in['b1'], 'L0_ffn_w2': _L0_ffn_in['w2'], 'L0_ffn_b2': _L0_ffn_in['b2']}

def reference(x, ctx_1024, g_xattn, g_ffn, L0_xattn_wq_w, L0_xattn_wq_b, L0_xattn_wk_w, L0_xattn_wk_b, L0_xattn_wv_w, L0_xattn_wv_b, L0_xattn_dense_w, L0_xattn_dense_b, L0_ffn_router_w, L0_ffn_w1, L0_ffn_b1, L0_ffn_w2, L0_ffn_b2):
    import jax
    import jax.numpy as jnp

    def _L0_xattn_ref(q, k, v, wq_w, wq_b, wk_w, wk_b, wv_w, wv_b, dense_w, dense_b):
        import jax, jax.numpy as jnp
        import numpy as np
        B, S, D, H = (4, 512, 256, 16)
        DEPTH = D // H
        NEG = -1000000000.0

        def _split_heads(x):
            b, s, _ = x.shape
            return x.reshape(b, s, H, DEPTH).transpose(0, 2, 1, 3)
        b, s, _ = q.shape
        qh = _split_heads(q @ wq_w.T + wq_b)
        kh = _split_heads(k @ wk_w.T + wk_b)
        vh = _split_heads(v @ wv_w.T + wv_b)
        logits = jnp.einsum('bhqd,bhkd->bhqk', qh, kh) / np.sqrt(DEPTH).astype(np.float32)
        mask = jnp.where(jnp.triu(jnp.ones((s, s), jnp.float32), k=1) == 1.0, NEG, 0.0)
        logits = logits + mask
        attn = jax.nn.softmax(logits, axis=-1)
        out = jnp.einsum('bhqk,bhkd->bhqd', attn, vh)
        out = out.transpose(0, 2, 1, 3).reshape(b, s, D)
        return out @ dense_w.T + dense_b

    def _L0_ffn_ref(h, router_w, w1, b1, w2, b2):
        import jax, jax.numpy as jnp
        import numpy as np
        B, S, D, E, F = (2, 512, 256, 14, 512)
        Bb, Ss, Dd = h.shape
        x = h.reshape(-1, Dd)
        logits = x @ router_w
        assignments = jnp.argmax(logits, axis=-1)
        probs = jax.nn.softmax(logits, axis=-1)
        weights = jnp.take_along_axis(probs, assignments[:, None], axis=1)[:, 0]
        hid = jnp.einsum('nd,edf->nef', x, w1) + b1
        hid = jax.nn.gelu(hid, approximate=False)
        all_out = jnp.einsum('nef,efd->ned', hid, w2) + b2
        sel = jnp.take_along_axis(all_out, assignments[:, None, None], axis=1)[:, 0, :]
        moe_out = (sel * weights[:, None]).reshape(Bb, Ss, Dd)
        return moe_out
    x = x + jnp.tanh(g_xattn[0]) * _L0_xattn_ref(_layernorm(x, axis=-1), ctx_1024, ctx_1024, L0_xattn_wq_w, L0_xattn_wq_b, L0_xattn_wk_w, L0_xattn_wk_b, L0_xattn_wv_w, L0_xattn_wv_b, L0_xattn_dense_w, L0_xattn_dense_b)
    x = x + jnp.tanh(g_ffn[0]) * _L0_ffn_ref(_layernorm(x, axis=-1), L0_ffn_router_w, L0_ffn_w1, L0_ffn_b1, L0_ffn_w2, L0_ffn_b2)
    return x

_drawn_inputs = setup_inputs


def setup_inputs(seed=0):
    import zlib

    import numpy as np

    out = dict(_drawn_inputs(seed))
    spreads = {'L0_ffn_b1': (0.0, 0.774), 'L0_ffn_b2': (0.0, 0.768)}
    factors = {'L0_xattn_wq_b': 8.0,
     'L0_xattn_wk_b': 8.0,
     'L0_xattn_wv_b': 4.397,
     'L0_xattn_dense_b': 4.153}
    for name, (base, spread) in spreads.items():
        noise = np.random.default_rng([zlib.crc32(name.encode()), seed]).standard_normal(out[name].shape)
        drawn = base * np.exp(spread * noise) if base else spread * noise
        out[name] = jnp.asarray(drawn.astype(out[name].dtype))
    for name, factor in factors.items():
        out[name] = (out[name] * factor).astype(out[name].dtype)
    return out
```

```python
from contextlib import ExitStack

import numpy as np
import concourse.bass as bass
from concourse import mybir

P = 128
B = 32
D = 256
DC = D // P
H = 16
DH = D // H
HQ = 4
QUADS = H // HQ
VW = DH + 1
E = 14
F = 512
FC = F // P
TOK = B * P
REGION = TOK + P
SLOTS = (TOK - E) // P + E
R = 5
IDLE_ROWS = (SLOTS - TOK // P) * P
ROW = 2 * D + 1
NEG = -1.0e9
EPS = 1e-5
NO_TOKEN = TOK
NAMES = E * REGION + IDLE_ROWS
RANK = D + 16

F32 = mybir.dt.float32
BF16 = mybir.dt.bfloat16
I32 = mybir.dt.int32
ALU = mybir.AluOpType
ACT = mybir.ActivationFunctionType
AX_X = mybir.AxisListType.X

CONST_COLS = {}


def build_constants():
    p = np.arange(P)[:, None]
    j = np.arange(P)[None, :]
    e = np.arange(E)[None, :]
    blocks = {
        "ident": (p == j),
        "causal": np.where(j > p, NEG, 0.0),
        "before": (p < j),
        "headmask": (p // DH) % HQ == np.arange(HQ)[None, :],
        "first": np.broadcast_to(16.0 - e, (P, E)),
        "region": np.broadcast_to(REGION * e, (P, E)),
        "slot": np.broadcast_to(np.arange(SLOTS)[None, :], (P, SLOTS)),
        "tile": np.broadcast_to(P * np.arange(B)[None, :], (P, B)),
        "select": (p % 32 == e) & (p < 96),
        "token": P * np.arange(B)[None, :] + p,
    }
    at = 0
    for name, block in blocks.items():
        CONST_COLS[name] = (at, at + block.shape[1])
        at += block.shape[1]
    return np.concatenate([np.asarray(b, dtype=np.float32) for b in blocks.values()], axis=1)


class Batch:

    def __init__(self, i, k):
        self.i, self.k = i, k
        self.n = i * 4 + k
        self.slot = k % 4
        self.par = k % 2
        self.round = i + k // 4
        self.static = isinstance(i, int)

    def ok(self, last=B - 1):
        return not self.static or 0 <= self.n <= last

    def back(self, k):
        return Batch(self.i, self.k - k)


def wait(eng, sem, value):
    if isinstance(value, int) and value <= 0:
        return
    eng.wait_ge(sem, value)


def run_steps(eng, step, deepest=7):
    first = -(-deepest // 4)
    for t in range(4 * first):
        step(Batch(0, t))
    with eng.Fori(first, B // 4) as i:
        for j in range(4):
            step(Batch(i, j))
    for t in range(B, B + deepest):
        step(Batch(B // 4, t - B))


def flamingo_kernel(nc, x, ctxt, gates, wq, wk, wv, wd, bqk, bv, bd, rw, w1, w2, b12, consts, out):
    token_rows = nc.dram_tensor("token_rows", [TOK + P, ROW], F32, kind="Internal").ap()
    token_names = nc.dram_tensor("token_names", [NAMES, 1], I32, kind="Internal").ap()
    x_view = x.rearrange("b s d -> s b d")
    out_rows = out.rearrange("b s d -> (b s) d")

    with ExitStack() as ctx:
        def sb(name, shape, dt=F32):
            return ctx.enter_context(nc.sbuf_tensor(name, shape, dt))

        def sem(name):
            return ctx.enter_context(nc.semaphore(name))

        W1 = sb("W1", [P, E, DC, F])
        W2 = sb("W2", [P, E, FC, D])
        C = sb("C", [P, consts.shape[1]])

        def const(name):
            a, b = CONST_COLS[name]
            return C[:, a:b]

        ident = const("ident")
        ident_bf = sb("ident_bf", [P, P], BF16)
        causal_bf = sb("causal_bf", [P, HQ, P], BF16)
        before_bf = sb("before_bf", [P, P], BF16)
        ones_bf = sb("ones_bf", [P, P], BF16)
        select_bf = sb("select_bf", [P, E, P], BF16)
        bias_parts = sb("bias_parts", [P, F + D], BF16)
        rows = sb("rows", [P, 4, ROW])
        gate_raw = sb("gate_raw", [P, 2])
        gate = sb("gate", [P, 2])
        half = sb("half", [P, 1])
        logits = sb("logits", [P, 4, E])
        onehot = sb("onehot", [P, 2, E], BF16)
        pair_seen = sb("pair_seen", [P, E], BF16)
        seen = sb("seen", [P, E], BF16)
        route_max = sb("route_max", [P, 2])
        route_eq = sb("route_eq", [P, 2, E])
        route_order = sb("route_order", [P, 2, E])
        route_pick = sb("route_pick", [P, 2])
        shifted = sb("shifted", [P, 2, E])
        exp_logits = sb("exp_logits", [P, 2, E])
        exp_sum = sb("exp_sum", [P, 2])
        exp_inv = sb("exp_inv", [P, 2])
        rank = sb("rank", [P, 2, E])
        rank_at = sb("rank_at", [P, 2, E])
        pos_f = sb("pos_f", [P, 2])
        pos = sb("pos", [P, 4], I32)
        token_no = sb("token_no", [P, 4], I32)
        stats = sb("stats", [P, 4, 6])
        moments = sb("moments", [P, 4, 2])
        rstd = sb("rstd", [P, 4, 2])
        stats2 = sb("stats2", [P, 4, 6])
        moments2 = sb("moments2", [P, 4, 2])
        rstd2 = sb("rstd2", [P, 4, 2])
        negmax = sb("negmax", [P, 2, H])
        rsum = sb("rsum", [P, H])

        ARENA = 14000
        arena = sb("arena", [P, ARENA])
        taken = [0]

        def part(n):
            taken[0] += n
            assert taken[0] <= ARENA, taken
            return arena[:, taken[0] - n:taken[0]]

        wq_sb = part(DC * D).rearrange("p (c n) -> p c n", c=DC)
        wk_sb = part(DC * D).rearrange("p (c n) -> p c n", c=DC)
        wv_sb = part(DC * D).rearrange("p (c n) -> p c n", c=DC)
        wd_sb = part(DC * D).rearrange("p (c n) -> p c n", c=DC)
        rw_sb = part(DC * E).rearrange("p (c n) -> p c n", c=DC)
        bqk_sb = part(2 * DC)
        bv_sb = part(DC)
        resid_bias = part(D)
        x_in = part(4 * D).rearrange("p (r d) -> p r d", r=4)
        c_in = part(4 * D).rearrange("p (r c s) -> p r c s", r=4, c=DC)
        x_biased = part(4 * D).rearrange("p (r d) -> p r d", r=4)
        xn = part(2 * D).rearrange("p (r d) -> p r d", r=2)
        xh_t = part(2 * 2 * D).rearrange("p (r c s) -> p r c s", r=2, c=4)
        q_t = part(2 * D).rearrange("p (r c s) -> p r c s", r=2, c=DC)
        k_t = part(D).rearrange("p (c s) -> p c s", c=DC)
        k_masked = part(2 * DC * HQ * P).rearrange("p (r c v s) -> p r c v s", r=2, c=DC, v=HQ)
        values = part(2 * H * VW).rearrange("p (r h w) -> p r h w", r=2, h=H)
        probs0 = taken[0]
        probs = part(QUADS * HQ * P).rearrange("p (q v k) -> p q v k", q=QUADS, v=HQ)
        probs_t = part(2 * HQ * P).rearrange("p (r v s) -> p r v s", r=2, v=HQ)
        attn = part(D)
        attn_t = part(D)
        bias_in = arena[:, probs0:probs0 + F + D]
        bias_rest = arena[:, probs0 + F + D:probs0 + 2 * (F + D)]
        bd_rep = attn_t
        bv_rep = probs_t[:, 0, 0:2, :]
        bias_mid = sb("bias_mid", [P, F + D], BF16)

        taken[0] = 0
        g_rows = part(R * ROW).rearrange("p (r n) -> p r n", r=R)
        g_xt = part(R * D).rearrange("p (r c s) -> p r c s", r=R, c=DC)
        hid = part(R * F).rearrange("p (r n) -> p r n", r=R)
        hid_t = part(R * F).rearrange("p (r c s) -> p r c s", r=R, c=FC)
        g_out = part(R * D).rearrange("p (r n) -> p r n", r=R)
        g_idx = part(R).bitcast(I32)
        fetch_idx = part(R).bitcast(I32)
        slot_expert = part(SLOTS).bitcast(I32)
        slot_rows = part(SLOTS).bitcast(I32)
        slot_names = part(SLOTS).bitcast(I32)
        t_a = part(SLOTS * E).rearrange("p (s e) -> p s e", s=SLOTS)
        t_b = part(SLOTS * E).rearrange("p (s e) -> p s e", s=SLOTS)
        t_cmp = part(E * B).rearrange("p (e j) -> p e j", e=E)
        t_cnt = part(E)
        t_tiles = part(E)
        t_cum = part(E)
        t_one = part(E)
        t_e = part(SLOTS)
        t_c = part(SLOTS)
        t_r = part(SLOTS)

        bank = [ctx.enter_context(nc.psum_tensor(f"bank{k}", [P, 512], F32)) for k in range(8)]

        hid_bank = [bank[k] for k in (0, 1, 2, 6, 7)]

        small_loaded = sem("small_loaded")
        bias_loaded = sem("bias_loaded")
        consts_loaded = sem("consts_loaded")
        attn_w_loaded = sem("attn_w_loaded")
        experts_loaded = sem("experts_loaded")
        x_loaded = [sem(f"x_loaded{r}") for r in range(4)]
        c_loaded = [sem(f"c_loaded{r}") for r in range(4)]
        idle_written = sem("idle_written")
        setup_pool = sem("setup_pool")
        bias_zeroed = sem("bias_zeroed")
        tanh_done = sem("tanh_done")
        consts_cast = sem("consts_cast")
        bv_spread = sem("bv_spread")
        out_bias_done = sem("out_bias_done")
        resid_bias_ready = sem("resid_bias_ready")
        idle_ready = sem("idle_ready")

        stats_done = sem("stats_done")
        moments_ready = sem("moments_ready")
        rstd_step = sem("rstd_step")
        xn_ready = sem("xn_ready")
        x_used = sem("x_used")
        xh_transposed = sem("xh_transposed")
        xh_ready = sem("xh_ready")
        qk_done = sem("qk_done")
        qk_ready = sem("qk_ready")
        k_masked_ready = sem("k_masked_ready")
        v_done = sem("v_done")
        values_ready = sem("values_ready")
        logits_ready = sem("logits_ready")
        rank_ready = sem("rank_ready")
        scores_ready = sem("scores_ready")
        max_ready = sem("max_ready")
        probs_ready = sem("probs_ready")
        probs_transposed = sem("probs_transposed")
        probs_t_ready = sem("probs_t_ready")
        av_done = sem("av_done")
        rsum_ready = sem("rsum_ready")
        token_written = sem("token_written")
        weight_ready = sem("weight_ready")
        wd_scaled = sem("wd_scaled")
        attn_ready = sem("attn_ready")
        attn_transposed = sem("attn_transposed")
        attn_t_ready = sem("attn_t_ready")
        dense_done = sem("dense_done")
        x2_ready = sem("x2_ready")
        stats2_done = sem("stats2_done")
        moments2_ready = sem("moments2_ready")
        rstd2_step = sem("rstd2_step")
        h_ready = sem("h_ready")
        route_step = sem("route_step")
        shifted_ready = sem("shifted_ready")
        onehot_ready = sem("onehot_ready")
        exp_logits_ready = sem("exp_logits_ready")
        rank_masked = sem("rank_masked")
        pos_summed = sem("pos_summed")
        seen_ready = sem("seen_ready")
        pos_ready = sem("pos_ready")
        row_stored = [sem(f"row_stored{r}") for r in range(4)]
        name_stored = [sem(f"name_stored{r}") for r in range(4)]
        names_loaded = [sem(f"names_loaded{r}") for r in range(R)]

        load_waits = sem("load_waits")
        pool_waits = sem("pool_waits")
        vector_waits = sem("vector_waits")
        counts_done = sem("counts_done")
        table_step = sem("table_step")
        tables_ready = sem("tables_ready")
        rows_fetched = [sem(f"rows_fetched{r}") for r in range(R)]
        fetch_named = sem("fetch_named")
        gx_transposed = sem("gx_transposed")
        gx_ready = sem("gx_ready")
        hid_done = sem("hid_done")
        hid_ready = sem("hid_ready")
        hid_transposed = sem("hid_transposed")
        hid_t_ready = sem("hid_t_ready")
        y_done = sem("y_done")
        out_ready = sem("out_ready")
        idx_ready = sem("idx_ready")
        out_stored = [sem(f"out_stored{r}") for r in range(R)]

        block = ctx.enter_context(nc.Block())

        @block.sync
        def _(sp):
            sp.dma_start(C[:, :], consts).then_inc(consts_loaded, 16)

            def hold(sem_, value):
                wait(sp, sem_, value)
                if not isinstance(value, int):
                    sp.sem_inc(load_waits, 1)

            def load(b):
                hold(x_used, b.n - 3)
                sp.dma_start(x_in[:, b.slot, :], x_view[:, bass.ds(b.n, 1), :]
                             .rearrange("s b d -> s (b d)")).then_inc(x_loaded[b.slot], 16)
                hold(v_done, b.n - 3)
                sp.dma_start(c_in[:, b.slot, :, :].rearrange("p c s -> p (c s)"),
                             ctxt[:, bass.ds(b.n, 1), :].rearrange("p b n -> p (b n)")
                             ).then_inc(c_loaded[b.slot], 16)

            def store(b):
                hold(h_ready, b.n + 1)
                hold(weight_ready, b.n + 1 + (1 - b.par))
                sp.dma_start(token_rows[bass.ds(b.n * P, P), :], rows[:, b.slot, :]).then_inc(row_stored[b.slot], 16)

            def step(t):
                b = t.back(9)
                if b.ok():
                    store(b)
                if t.ok():
                    load(t)
                if t.static and t.n == 0:
                    for dst, src in ((wq_sb, wq), (wk_sb, wk), (wv_sb, wv), (wd_sb, wd), (rw_sb, rw)):
                        sp.dma_start(dst, src).then_inc(attn_w_loaded, 16)

            run_steps(sp, step, deepest=9)

            for r in range(4):
                hold(name_stored[r], 16 * (B // 4) + 16)
            hold(tables_ready, 1)

            def load_names(r, s):
                row = sp.value_load(slot_rows[0:1, bass.ds(s, 1)], min_val=0, max_val=NAMES - P)
                sp.dma_start(slot_names[:, bass.ds(s, 1)], token_names[bass.ds(row, P), :]
                             ).then_inc(names_loaded[r], 16)

            for k in range(R):
                load_names(k, k)
            with sp.Fori(1, SLOTS // R) as i:
                for k in range(R):
                    hold(names_loaded[k], i * 16)
                    load_names(k, i * R + k)

        @block.gpsimd
        def _(pool):
            done = [0]

            def link(ins):
                done[0] += 1
                ins.then_inc(setup_pool, 1)
                pool.wait_ge(setup_pool, done[0])

            pool.memset(half[:, :], -0.5)
            pool.memset(values, 1.0)
            pool.memset(seen[:, :], 0.0)
            pool.memset(ones_bf[:, :], 1.0)
            link(pool.memset(rows[:, 3, :], 0.0))
            pool.dma_start(token_rows[TOK:TOK + P, :], rows[:, 3, :]).then_inc(idle_written, 16)
            no_names = probs.rearrange("p q v k -> p (q v k)").bitcast(I32)[:, 2 * (F + D):2 * (F + D) + NAMES // P]
            link(pool.memset(no_names, NO_TOKEN))
            blank = token_names.rearrange("(p n) o -> p (n o)", p=P)
            for r in range(4):
                n = slice(r * NAMES // P // 4, (r + 1) * NAMES // P // 4)
                pool.dma_start(blank[:, n], no_names[:, n]).then_inc(name_stored[r], 16)
            link(pool.memset(bias_in, 0.0))
            for g in range(3):
                pool.dma_start(bias_in[32 * g:32 * g + E, :], b12).then_inc(bias_loaded, 16)
            pool.wait_ge(bias_loaded, 48)
            link(pool.tensor_copy(bias_parts[:, :], bias_in))
            link(pool.tensor_tensor(bias_rest, bias_in, bias_parts[:, :], ALU.subtract))
            link(pool.tensor_copy(bias_mid[:, :], bias_rest))
            link(pool.tensor_copy(bias_parts[32:64, :], bias_mid[32:64, :]))
            link(pool.tensor_tensor(bias_rest, bias_rest, bias_mid[:, :], ALU.subtract))
            link(pool.tensor_copy(bias_parts[64:96, :], bias_rest[64:96, :]))
            pool.wait_ge(idle_written, 16)
            for r in range(4):
                pool.wait_ge(name_stored[r], 16)
            pool.wait_ge(consts_loaded, 16)
            pool.wait_ge(resid_bias_ready, 1)

            def hold(sem_, value):
                wait(pool, sem_, value)
                if not isinstance(value, int):
                    pool.sem_inc(pool_waits, 1)

            def norm(b, var, rs, counter):
                pool.tensor_scalar(rs[:, b.slot, 0:1], var, EPS, None, ALU.add).then_inc(counter, 1)
                hold(counter, b.n * 2 + 1)
                pool.tensor_tensor(rs[:, b.slot, 1:2], rs[:, b.slot, 0:1], half[:, :], ALU.pow).then_inc(counter, 1)
                hold(counter, b.n * 2 + 2)

            def step(t):
                a, a1, c, f = t, t.back(1), t.back(3), t.back(6)
                if a.ok():
                    hold(moments_ready, a.n + 1)
                    norm(a, moments[:, a.slot, 1:2], rstd, rstd_step)
                    hold(xh_transposed, a.n - 1)
                    pool.tensor_scalar(xn[:, a.par, :], x_in[:, a.slot, :], moments[:, a.slot, 0:1],
                                       rstd[:, a.slot, 1:2], ALU.subtract, ALU.mult).then_inc(xn_ready, 1)
                    hold(x2_ready, a.n - 3)
                    pool.tensor_tensor(x_biased[:, a.slot, :], x_in[:, a.slot, :], resid_bias,
                                       ALU.add).then_inc(x_used, 1)
                if f.ok() and f.par == 1:
                    for b in (f.back(1), f):
                        hold(name_stored[b.slot], b.round * 16 + 16)
                        pool.tensor_copy(token_no[:, b.slot:b.slot + 1],
                                         const("token")[:, bass.ds(b.n, 1)]).then_inc(token_written, 1)
                    hold(token_written, f.n + 1)
                    hold(pos_ready, f.n + 1)
                    for b in (f.back(1), f):
                        pool.indirect_dma_start(
                            out=token_names, out_offset=bass.IndirectOffsetOnAxis(ap=pos[:, b.slot:b.slot + 1], axis=0),
                            in_=token_no[:, b.slot:b.slot + 1], in_offset=None).then_inc(name_stored[b.slot], 16)
                if c.ok():
                    hold(moments2_ready, c.n + 1)
                    norm(c, moments2[:, c.slot, 1:2], rstd2, rstd2_step)
                    pool.tensor_scalar(rows[:, c.slot, 0:D], rows[:, c.slot, D:2 * D],
                                       moments2[:, c.slot, 0:1], rstd2[:, c.slot, 1:2],
                                       ALU.subtract, ALU.mult).then_inc(h_ready, 1)
                if a1.ok():
                    hold(qk_ready, a1.n + 1)
                    hold(scores_ready, a1.n * 4 - 4)
                    for ch in range(DC):
                        ins = pool.tensor_tensor(
                            k_masked[:, a1.par, ch, :, :],
                            k_t[:, ch, :].rearrange("p (o s) -> p o s", o=1).to_broadcast([P, HQ, P]),
                            const("headmask").rearrange("p (v o) -> p v o", o=1).to_broadcast([P, HQ, P]),
                            ALU.mult)
                    ins.then_inc(k_masked_ready, 1)

            run_steps(pool, step)

            for r in range(4):
                hold(row_stored[r], 16 * (B // 4))
            hold(tables_ready, 1)

            def fetch(r, s, rnd):
                hold(names_loaded[r], rnd * 16 + 16)
                pool.tensor_copy(fetch_idx[:, r:r + 1], slot_names[:, bass.ds(s, 1)]).then_inc(fetch_named, 1)
                hold(fetch_named, s + 1)
                pool.indirect_dma_start(
                    out=g_rows[:, r, :], out_offset=None, in_=token_rows,
                    in_offset=bass.IndirectOffsetOnAxis(ap=fetch_idx[:, r:r + 1], axis=0)
                ).then_inc(rows_fetched[r], 16)

            def store(r, s):
                hold(idx_ready, s + 1)
                hold(out_ready, s + 1)
                pool.indirect_dma_start(
                    out=out_rows, out_offset=bass.IndirectOffsetOnAxis(ap=g_idx[:, r:r + 1], axis=0),
                    in_=g_out[:, r, :], in_offset=None, bounds_check=TOK - 1, oob_is_err=False
                ).then_inc(out_stored[r], 16)

            for k in range(R):
                fetch(k, k, 0)
            with pool.Fori(0, SLOTS // R - 1) as i:
                for k in range(R):
                    store(k, i * R + k)
                    fetch(k, i * R + (k + R), i + 1)
            for k in range(R):
                store(k, SLOTS - R + k)
            for k in range(R):
                pool.wait_ge(out_stored[k], 16 * (SLOTS // R))

        @block.scalar
        def _(act):
            act.dma_start(gate_raw[:, :], gates.to_broadcast([P, 2])).then_inc(small_loaded, 16)
            act.dma_start(bqk_sb, bqk).then_inc(small_loaded, 16)
            act.dma_start(bv_sb, bv).then_inc(small_loaded, 16)
            act.dma_start(bd_rep, bd.to_broadcast([P, D])).then_inc(small_loaded, 16)
            for e in range(E):
                act.dma_start(W1[:, e, :, :].rearrange("p c n -> p (c n)"), w1[e]).then_inc(experts_loaded, 16)
                act.dma_start(W2[:, e, :, :].rearrange("p c n -> p (c n)"), w2[e]).then_inc(experts_loaded, 16)
            act.wait_ge(small_loaded, 64)
            act.activation(gate[:, :], gate_raw[:, :], ACT.Tanh).then_inc(tanh_done, 1)

            def step(t):
                a1, b, d, e = t.back(1), t.back(2), t.back(4), t.back(5)
                if b.ok():
                    for q in range(QUADS):
                        act.wait_ge(max_ready, b.n * 4 + (q + 1))
                        wait(act, probs_transposed, b.n * 4 + (q - 3))
                        for v in range(HQ):
                            h = q * HQ + v
                            ins = act.activation(probs[:, q, v, :], bank[q][:, v * P:(v + 1) * P], ACT.Exp,
                                                 bias=negmax[:, b.par, h:h + 1])
                        ins.then_inc(probs_ready, 1)
                if e.ok() and e.par == 1:
                    act.wait_ge(shifted_ready, e.n + 1)
                    act.activation(exp_logits[:, :, :], shifted[:, :, :], ACT.Exp).then_inc(exp_logits_ready, 2)
                if a1.ok():
                    act.wait_ge(v_done, t.n)
                    wait(act, av_done, a1.n * 4 - 4)
                    act.activation(values[:, a1.par, :, 0:DH], bank[6][:, 0:D].rearrange("p (h w) -> p h w", h=H),
                                   ACT.Copy).then_inc(values_ready, 1)
                if d.ok():
                    act.wait_ge(v_done, t.n)
                    act.activation(logits[:, d.slot, :], bank[6][:, D:D + E], ACT.Copy).then_inc(logits_ready, 1)
                if e.ok() and e.par == 1:
                    act.wait_ge(v_done, t.n)
                    act.activation(rank[:, :, :], bank[6][:, RANK:RANK + 2 * E].rearrange("p (r e) -> p r e", r=2),
                                   ACT.Copy).then_inc(rank_ready, 2)

            run_steps(act, step)

            def gelu(k, s):
                act.wait_ge(hid_done, s + 1)
                act.activation(hid[:, k, :], hid_bank[k][:, :], ACT.Gelu).then_inc(hid_ready, 1)

            with act.Fori(0, SLOTS // R) as i:
                for k in range(R):
                    gelu(k, i * R + k)

        @block.vector
        def _(dve):
            dve.wait_ge(consts_loaded, 16)
            dve.tensor_copy(ident_bf[:, :], ident)
            dve.tensor_copy(causal_bf[:, :, :], const("causal").rearrange("p (o k) -> p o k", o=1)
                            .to_broadcast([P, HQ, P]))
            dve.tensor_copy(before_bf[:, :], const("before"))
            dve.tensor_copy(select_bf[:, :, :], const("select").rearrange("p (e o) -> p e o", o=1)
                            .to_broadcast([P, E, P])).then_inc(consts_cast, 1)
            dve.wait_ge(small_loaded, 64)
            dve.tensor_copy(bv_rep, bv_sb.rearrange("p (c o) -> p c o", o=1).to_broadcast([P, DC, P])
                            ).then_inc(bv_spread, 1)
            dve.wait_ge(out_bias_done, 1)
            dve.tensor_tensor(resid_bias, bank[7][:, 0:D], bd_rep, ALU.add).then_inc(bv_spread, 1)
            dve.wait_ge(bv_spread, 2)
            dve.wait_ge(tanh_done, 1)
            dve.tensor_scalar(resid_bias, resid_bias, gate[:, 0:1], None, ALU.mult).then_inc(resid_bias_ready, 1)
            dve.tensor_scalar(wd_sb, wd_sb, gate[:, 0:1], None, ALU.mult).then_inc(wd_scaled, 1)

            def step(t):
                a, a1, b, c, d, e = t, t.back(1), t.back(2), t.back(3), t.back(4), t.back(5)
                routes = e.ok() and e.par == 1

                def maxima(q):
                    dve.wait_ge(scores_ready, b.n * 4 + (q + 1))
                    dve.tensor_reduce(negmax[:, b.par, q * HQ:(q + 1) * HQ],
                                      bank[q][:, :].rearrange("p (v k) -> p v k", v=HQ),
                                      axis=AX_X, op=ALU.max, negate=True).then_inc(max_ready, 1)

                def transposed_probs(q):
                    dve.wait_ge(probs_transposed, b.n * 4 + (q + 1))
                    wait(dve, av_done, b.n * 4 + (q - 1))
                    dve.tensor_copy(probs_t[:, q % 2, :, :].rearrange("p v s -> p (v s)"),
                                    bank[4 + q % 2][:, :]).then_inc(probs_t_ready, 1)

                if a.ok():
                    dve.wait_ge(x_loaded[a.slot], (a.round + 1) * 16)
                    dve.bn_stats(stats[:, a.slot, :], x_in[:, a.slot, :]).then_inc(stats_done, 1)
                    dve.wait_ge(stats_done, a.n + 1)
                    dve.sem_inc(vector_waits, 1)
                    dve.bn_aggr(moments[:, a.slot, :], stats[:, a.slot, :]).then_inc(moments_ready, 1)
                if b.ok():
                    maxima(0)
                    maxima(1)
                if c.ok():
                    dve.wait_ge(av_done, c.n * 4 + 4)
                    wait(dve, attn_transposed, c.n)
                    av = bank[7][:, 0:H * VW].rearrange("p (h w) -> p h w", h=H)
                    dve.reciprocal(rsum[:, :], av[:, :, DH]).then_inc(rsum_ready, 1)
                    dve.wait_ge(rsum_ready, c.n + 1)
                    dve.tensor_tensor(attn.rearrange("p (h w) -> p h w", h=H), av[:, :, 0:DH],
                                      rsum[:, :].rearrange("p (h o) -> p h o", o=1).to_broadcast([P, H, DH]),
                                      ALU.mult).then_inc(attn_ready, 1)
                if b.ok():
                    maxima(2)
                    maxima(3)
                if c.ok():
                    dve.wait_ge(attn_transposed, c.n + 1)
                    wait(dve, dense_done, c.n)
                    dve.tensor_copy(attn_t, bank[4][:, 0:D]).then_inc(attn_t_ready, 1)
                if a1.ok() or d.ok():
                    lo, hi = (0 if a1.ok() else DC), (4 if d.ok() else DC)
                    dve.wait_ge(xh_transposed, t.n)
                    wait(dve, v_done, t.n - 2)
                    dve.tensor_copy(xh_t[:, t.par, lo:hi, :].rearrange("p c s -> p (c s)"),
                                    bank[6][:, lo * P:hi * P]).then_inc(xh_ready, 1)
                if c.ok():
                    dve.wait_ge(dense_done, c.n + 1)
                    dve.wait_ge(x_used, c.n + 1)
                    wait(dve, row_stored[c.slot], c.round * 16)
                    dve.tensor_tensor(rows[:, c.slot, D:2 * D], bank[5][:, 0:D], x_biased[:, c.slot, :],
                                      ALU.add).then_inc(x2_ready, 1)
                    dve.wait_ge(x2_ready, c.n + 1)
                    dve.bn_stats(stats2[:, c.slot, :], rows[:, c.slot, D:2 * D]).then_inc(stats2_done, 1)
                    dve.wait_ge(stats2_done, c.n + 1)
                    dve.sem_inc(vector_waits, 1)
                    dve.bn_aggr(moments2[:, c.slot, :], stats2[:, c.slot, :]).then_inc(moments2_ready, 1)
                if b.ok():
                    transposed_probs(0)
                if a1.ok():
                    dve.wait_ge(qk_done, a1.n + 1)
                    wait(dve, scores_ready, a1.n * 4 - 4)
                    wait(dve, k_masked_ready, a1.n)
                    for ch in range(DC):
                        dve.tensor_scalar(q_t[:, a1.par, ch, :], bank[6][:, ch * P:(ch + 1) * P],
                                          bqk_sb[:, ch:ch + 1], float(DH) ** -0.5, ALU.add, ALU.mult)
                    for ch in range(DC):
                        ins = dve.tensor_scalar(k_t[:, ch, :], bank[6][:, (DC + ch) * P:(DC + ch + 1) * P],
                                                bqk_sb[:, DC + ch:DC + ch + 1], None, ALU.add)
                    ins.then_inc(qk_ready, 1)
                if b.ok():
                    transposed_probs(1)
                if routes:
                    pair = logits[:, e.slot - 1:e.slot + 1, :]
                    base = (e.n - 1) * 4
                    dve.wait_ge(logits_ready, e.n + 1)
                    dve.tensor_reduce(route_max[:, :], pair, axis=AX_X, op=ALU.max).then_inc(route_step, 1)
                    dve.wait_ge(route_step, base + 1)
                    top = route_max[:, :].rearrange("p (r o) -> p r o", o=1).to_broadcast([P, 2, E])
                    dve.tensor_tensor(route_eq[:, :, :], pair, top, ALU.is_equal).then_inc(route_step, 1)
                    dve.tensor_tensor(shifted[:, :, :], pair, top, ALU.subtract).then_inc(shifted_ready, 2)
                    dve.wait_ge(route_step, base + 2)
                    dve.tensor_tensor(route_order[:, :, :], route_eq[:, :, :],
                                      const("first").rearrange("p (o e) -> p o e", o=1).to_broadcast([P, 2, E]),
                                      ALU.mult).then_inc(route_step, 1)
                    dve.wait_ge(route_step, base + 3)
                    dve.tensor_reduce(route_pick[:, :], route_order[:, :, :], axis=AX_X,
                                      op=ALU.max).then_inc(route_step, 1)
                    dve.wait_ge(route_step, base + 4)
                    dve.tensor_tensor(onehot[:, :, :], route_order[:, :, :],
                                      route_pick[:, :].rearrange("p (r o) -> p r o", o=1).to_broadcast([P, 2, E]),
                                      ALU.is_equal).then_inc(onehot_ready, 2)
                if b.ok():
                    transposed_probs(2)
                    transposed_probs(3)
                if routes:
                    dve.wait_ge(exp_logits_ready, e.n + 1)
                    dve.tensor_reduce(exp_sum[:, :], exp_logits[:, :, :], axis=AX_X,
                                      op=ALU.add).then_inc(route_step, 1)
                    dve.wait_ge(onehot_ready, e.n + 1)
                    dve.tensor_tensor(pair_seen[:, :], onehot[:, 0, :], onehot[:, 1, :],
                                      ALU.add).then_inc(route_step, 1)
                    dve.wait_ge(route_step, base + 5)
                    dve.reciprocal(exp_inv[:, :], exp_sum[:, :]).then_inc(route_step, 1)
                    dve.wait_ge(route_step, base + 6)
                    dve.wait_ge(rank_ready, e.n + 1)
                    dve.tensor_tensor(seen[:, :], seen[:, :], pair_seen[:, :], ALU.add).then_inc(seen_ready, 2)
                    dve.wait_ge(route_step, base + 7)
                    dve.tensor_scalar(rows[:, e.slot - 1:e.slot + 1, 2 * D],
                                      exp_inv[:, :], gate[:, 1:2], None, ALU.mult).then_inc(weight_ready, 2)
                    dve.tensor_tensor(rank_at[:, :, :], rank[:, :, :],
                                      const("region").rearrange("p (o e) -> p o e", o=1).to_broadcast([P, 2, E]),
                                      ALU.add).then_inc(route_step, 1)
                    dve.wait_ge(route_step, base + 8)
                    dve.tensor_tensor(rank_at[:, :, :], rank_at[:, :, :], onehot[:, :, :],
                                      ALU.mult).then_inc(rank_masked, 2)
                    dve.wait_ge(rank_masked, e.n + 1)
                    dve.tensor_reduce(pos_f[:, :], rank_at[:, :, :], axis=AX_X,
                                      op=ALU.add).then_inc(pos_summed, 2)
                    dve.wait_ge(pos_summed, e.n + 1)
                    for n in (e.back(1), e):
                        wait(dve, name_stored[n.slot], n.round * 16 + 16)
                    dve.tensor_copy(pos[:, e.slot - 1:e.slot + 1], pos_f[:, :]).then_inc(pos_ready, 2)

            run_steps(dve, step)

            done = [0]

            def link(ins):
                done[0] += 1
                ins.then_inc(table_step, 1)
                dve.wait_ge(table_step, done[0])

            def over_e(ap, n):
                return ap.rearrange("p (s o) -> p s o", o=1).to_broadcast([P, n, E])

            def over_s(ap):
                return ap.rearrange("p (o e) -> p o e", o=1).to_broadcast([P, SLOTS, E])

            dve.wait_ge(counts_done, 1)
            dve.memset(t_one, 1.0)
            link(dve.tensor_copy(t_cnt, bank[7][:, 0:E]))
            link(dve.tensor_tensor(t_cmp, t_cnt.rearrange("p (e o) -> p e o", o=1).to_broadcast([P, E, B]),
                                   const("tile").rearrange("p (o j) -> p o j", o=1).to_broadcast([P, E, B]),
                                   ALU.is_gt))
            link(dve.tensor_reduce(t_tiles, t_cmp, axis=AX_X, op=ALU.add))
            link(dve.tensor_tensor_scan(t_cum, t_one, t_tiles, 0.0, ALU.mult, ALU.add))
            link(dve.tensor_tensor(t_a, over_s(t_cum), over_e(const("slot"), SLOTS), ALU.is_le))
            dve.tensor_reduce(t_e, t_a, axis=AX_X, op=ALU.add)
            link(dve.tensor_tensor(t_b, over_s(t_cum), t_a, ALU.mult))
            link(dve.tensor_reduce(t_c, t_b, axis=AX_X, op=ALU.max))
            link(dve.tensor_tensor(t_c, const("slot"), t_c, ALU.subtract))
            link(dve.tensor_scalar(t_c, t_c, float(P), None, ALU.mult))
            link(dve.tensor_scalar(t_r, t_e, float(REGION), None, ALU.mult))
            link(dve.tensor_tensor(t_r, t_r, t_c, ALU.add))
            dve.tensor_copy(slot_rows, t_r)
            link(dve.tensor_scalar(t_e, t_e, float(E - 1), None, ALU.min))
            dve.tensor_copy(slot_expert, t_e).then_inc(tables_ready, 1)

            def up(r, s):
                dve.wait_ge(gx_transposed, s + 1)
                dve.tensor_copy(g_xt[:, r, :, :].rearrange("p c s -> p (c s)"), bank[3][:, 0:D]).then_inc(gx_ready, 1)

            def down(r, s):
                dve.wait_ge(hid_transposed, s + 1)
                dve.tensor_copy(hid_t[:, r, :, :].rearrange("p c s -> p (c s)"), bank[4][:, :]).then_inc(hid_t_ready, 1)

            def result(r, s, rnd):
                wait(dve, out_stored[r], rnd * 16)
                dve.tensor_copy(g_idx[:, r:r + 1], slot_names[:, bass.ds(s, 1)]).then_inc(idx_ready, 1)
                dve.wait_ge(y_done, s + 1)
                dve.scalar_tensor_tensor(g_out[:, r, :], bank[5][:, 0:D], g_rows[:, r, 2 * D:2 * D + 1],
                                         g_rows[:, r, D:2 * D], ALU.mult, ALU.add).then_inc(out_ready, 1)

            def slot(k, s, rnd, ahead=True):
                down(k, s)
                if ahead:
                    up((k + 2) % R, s + 2)
                result(k, s, rnd)

            up(0, 0)
            up(1, 1)
            for k in range(R):
                slot(k, k, 0)
            with dve.Fori(1, SLOTS // R - 1) as i:
                for k in range(R):
                    slot(k, i * R + k, i)
            for k in range(R):
                slot(k, SLOTS - R + k, SLOTS // R - 1, ahead=k + 2 < R)

        @block.tensor
        def _(pe):
            pe.wait_ge(attn_w_loaded, 16 * 5)
            pe.wait_ge(bv_spread, 1)
            for ch in range(DC):
                ins = pe.matmul(bank[7][:, 0:D], bv_rep[:, ch, :], wd_sb[:, ch, :], start=(ch == 0), stop=(ch == DC - 1))
            ins.then_inc(out_bias_done, 1)
            pe.wait_ge(resid_bias_ready, 1)
            pe.wait_ge(consts_cast, 1)
            pe.wait_ge(wd_scaled, 1)

            def step(t):
                a1, b, c, d, e = t.back(1), t.back(2), t.back(3), t.back(4), t.back(5)

                def scores(ch):
                    for r in range(2):
                        q = 2 * ch + r
                        wait(pe, probs_ready, b.n * 4 + (q - 3))
                        pe.matmul(bank[q][:, :], ident_bf[:, :], causal_bf[:, :, :].rearrange("p v k -> p (v k)"),
                                  start=True, stop=False)
                    for r in range(2):
                        q = 2 * ch + r
                        g = slice(64 * r, 64 * r + 64)
                        pe.matmul(bank[q][:, :], q_t[g, b.par, ch, :],
                                  k_masked[g, b.par, ch, :, :].rearrange("p v k -> p (v k)"),
                                  start=False, stop=True).then_inc(scores_ready, 1)

                def transpose_probs(q):
                    pe.wait_ge(probs_ready, b.n * 4 + (q + 1))
                    for v in range(HQ):
                        ins = pe.transpose(bank[4 + q % 2][:, v * P:(v + 1) * P], probs[:, q, v, :], ident)
                    ins.then_inc(probs_transposed, 1)

                def attend(n, q):
                    pe.wait_ge(probs_t_ready, n.n * 4 + (q + 1))
                    for v in range(HQ):
                        h = q * HQ + v
                        ins = pe.matmul(bank[7][:, h * VW:(h + 1) * VW], probs_t[:, q % 2, v, :],
                                        values[:, n.par, h, :], start=True, stop=True)
                    ins.then_inc(av_done, 1)

                if b.ok():
                    pe.wait_ge(k_masked_ready, b.n + 1)
                    scores(0)
                if c.ok():
                    attend(c, 3)
                if b.ok():
                    scores(1)
                if c.ok():
                    pe.wait_ge(attn_ready, c.n + 1)
                    pe.wait_ge(probs_t_ready, c.n * 4 + 4)
                    for ch in range(DC):
                        ins = pe.transpose(bank[4][:, ch * P:(ch + 1) * P], attn[:, ch * P:(ch + 1) * P], ident)
                    ins.then_inc(attn_transposed, 1)
                if a1.ok() or d.ok():
                    if t.back(2).ok():
                        pe.wait_ge(values_ready, t.n - 1)
                    if t.back(5).ok():
                        pe.wait_ge(logits_ready, t.n - 4)
                    if t.back(6).ok() and t.back(6).par == 1:
                        pe.wait_ge(rank_ready, t.n - 5)
                    if a1.ok():
                        pe.wait_ge(xn_ready, a1.n + 1)
                        for ch in range(DC):
                            ins = pe.transpose(bank[6][:, ch * P:(ch + 1) * P], xn[:, a1.par, ch * P:(ch + 1) * P], ident)
                    if d.ok():
                        pe.wait_ge(h_ready, d.n + 1)
                        for ch in range(DC):
                            ins = pe.transpose(bank[6][:, (DC + ch) * P:(DC + ch + 1) * P],
                                               rows[:, d.slot, ch * P:(ch + 1) * P], ident)
                    ins.then_inc(xh_transposed, 1)
                if c.ok():
                    pe.wait_ge(attn_t_ready, c.n + 1)
                    for ch in range(DC):
                        ins = pe.matmul(bank[5][:, 0:D], attn_t[:, ch * P:(ch + 1) * P], wd_sb[:, ch, :],
                                        start=(ch == 0), stop=(ch == DC - 1))
                    ins.then_inc(dense_done, 1)
                if b.ok():
                    transpose_probs(0)
                if a1.ok():
                    pe.wait_ge(xh_ready, t.n)
                    pe.wait_ge(c_loaded[a1.slot], (a1.round + 1) * 16)
                    for k, w in enumerate((wq_sb, wk_sb)):
                        for half_ in range(DC):
                            at = (k * DC + half_) * P
                            for ch in range(DC):
                                src = xh_t[:, t.par, ch, :] if k == 0 else c_in[:, a1.slot, ch, :]
                                ins = pe.matmul(bank[6][:, at:at + P], w[:, ch, half_ * P:(half_ + 1) * P], src,
                                                start=(ch == 0), stop=(ch == DC - 1))
                    ins.then_inc(qk_done, 1)
                if b.ok():
                    if c.ok():
                        pe.wait_ge(x2_ready, c.n + 1)
                    transpose_probs(1)
                    attend(b, 0)
                    transpose_probs(2)
                    attend(b, 1)
                if 1 <= t.k or not t.static or t.i > 0:
                    ins = None
                    if a1.ok():
                        pe.wait_ge(qk_ready, a1.n + 1)
                        for ch in range(DC):
                            ins = pe.matmul(bank[6][:, 0:D], c_in[:, a1.slot, ch, :], wv_sb[:, ch, :],
                                            start=(ch == 0), stop=(ch == DC - 1))
                    if d.ok():
                        pe.wait_ge(xh_ready, t.n)
                        for ch in range(DC):
                            ins = pe.matmul(bank[6][:, D:D + E], xh_t[:, t.par, DC + ch, :], rw_sb[:, ch, :],
                                            start=(ch == 0), stop=(ch == DC - 1))
                    if e.ok() and e.par == 1:
                        pe.wait_ge(onehot_ready, e.n + 1)
                        wait(pe, seen_ready, e.n - 1)
                        at = bank[6][:, RANK:RANK + 2 * E]
                        pe.matmul(at, before_bf[:, :], onehot[:, :, :].rearrange("p r e -> p (r e)"),
                                  start=True, stop=False)
                        pe.matmul(at[:, E:2 * E], ones_bf[:, :], onehot[:, 0, :], start=False, stop=False)
                        for r in range(2):
                            ins = pe.matmul(at[:, r * E:(r + 1) * E], ones_bf[:, :], seen[:, :],
                                            start=False, stop=(r == 1))
                    if ins is not None:
                        ins.then_inc(v_done, 1)
                if b.ok():
                    transpose_probs(3)
                    attend(b, 2)

            run_steps(pe, step)

            pe.wait_ge(seen_ready, B)
            pe.matmul(bank[7][:, 0:E], ones_bf[:, :], seen[:, :], start=True, stop=True).then_inc(counts_done, 1)
            pe.wait_ge(tables_ready, 1)
            pe.wait_ge(experts_loaded, 16 * 2 * E)

            def up_in(r, s, rnd):
                pe.wait_ge(rows_fetched[r], rnd * 16 + 16)
                if not (isinstance(s, int) and s == 0):
                    pe.wait_ge(gx_ready, s)
                for ch in range(DC):
                    ins = pe.transpose(bank[3][:, ch * P:(ch + 1) * P], g_rows[:, r, ch * P:(ch + 1) * P], ident)
                ins.then_inc(gx_transposed, 1)

            def expert(s):
                return pe.value_load(slot_expert[0:1, bass.ds(s, 1)], min_val=0, max_val=E - 1)

            def up(r, s):
                ex = expert(s)
                pe.wait_ge(gx_ready, s + 1)
                pe.matmul(hid_bank[r][:, :], select_bf[:, bass.ds(ex, 1), :].rearrange("p e s -> p (e s)"),
                          bias_parts[:, 0:F], start=True, stop=False)
                for ch in range(DC):
                    ins = pe.matmul(hid_bank[r][:, :], g_xt[:, r, ch, :],
                                    W1[:, bass.ds(ex, 1), ch, :].rearrange("p e n -> p (e n)"),
                                    start=False, stop=(ch == DC - 1))
                ins.then_inc(hid_done, 1)

            def down_in(r, s):
                pe.wait_ge(hid_ready, s + 1)
                if not (isinstance(s, int) and s == 0):
                    pe.wait_ge(hid_t_ready, s)
                for ch in range(FC):
                    ins = pe.transpose(bank[4][:, ch * P:(ch + 1) * P], hid[:, r, ch * P:(ch + 1) * P], ident)
                ins.then_inc(hid_transposed, 1)

            def down(r, s):
                ex = expert(s)
                pe.wait_ge(hid_t_ready, s + 1)
                if not (isinstance(s, int) and s == 0):
                    pe.wait_ge(out_ready, s)
                pe.matmul(bank[5][:, 0:D], select_bf[:, bass.ds(ex, 1), :].rearrange("p e s -> p (e s)"),
                          bias_parts[:, F:F + D], start=True, stop=False)
                for ch in range(FC):
                    ins = pe.matmul(bank[5][:, 0:D], hid_t[:, r, ch, :],
                                    W2[:, bass.ds(ex, 1), ch, :].rearrange("p e n -> p (e n)"),
                                    start=False, stop=(ch == FC - 1))
                ins.then_inc(y_done, 1)

            def slot(k, s, rnd, left=R):
                down_in(k, s)
                if left > 2:
                    up_in((k + 2) % R, s + 2, rnd + (k + 2) // R)
                if left > 1:
                    up((k + 1) % R, s + 1)
                down(k, s)

            up_in(0, 0, 0)
            up_in(1, 1, 0)
            up(0, 0)
            for k in range(R):
                slot(k, k, 0)
            with pe.Fori(1, SLOTS // R - 1) as i:
                for k in range(R):
                    slot(k, i * R + k, i)
            for k in range(R):
                slot(k, SLOTS - R + k, SLOTS // R - 1, left=R - k)


def kernel(x, ctx_1024, g_xattn, g_ffn, L0_xattn_wq_w, L0_xattn_wq_b, L0_xattn_wk_w, L0_xattn_wk_b,
           L0_xattn_wv_w, L0_xattn_wv_b, L0_xattn_dense_w, L0_xattn_dense_b, L0_ffn_router_w,
           L0_ffn_w1, L0_ffn_b1, L0_ffn_w2, L0_ffn_b2):
    import concourse.bacc as bacc
    from concourse.bass_utils import run_bass_kernel_spmd

    def in_chunks(w):
        return np.asarray(w).reshape(-1, P, w.shape[-1]).transpose(1, 0, 2)

    def column(v):
        return np.asarray(v).reshape(-1, P).T

    arrays = {
        "x": x,
        "ctxt": np.asarray(ctx_1024).reshape(B, P, DC, P).transpose(3, 0, 2, 1).reshape(P, B, DC * P),
        "gates": np.concatenate([np.asarray(g_xattn), np.asarray(g_ffn)]).reshape(1, 2),
        "wq": in_chunks(np.asarray(L0_xattn_wq_w).T),
        "wk": in_chunks(np.asarray(L0_xattn_wk_w).T),
        "wv": in_chunks(np.asarray(L0_xattn_wv_w).T),
        "wd": in_chunks(np.asarray(L0_xattn_dense_w).T),
        "bqk": np.concatenate([column(L0_xattn_wq_b), column(L0_xattn_wk_b)], axis=1),
        "bv": column(L0_xattn_wv_b),
        "bd": np.asarray(L0_xattn_dense_b).reshape(1, D),
        "rw": in_chunks(L0_ffn_router_w),
        "w1": np.asarray(L0_ffn_w1).reshape(E, DC, P, F).transpose(0, 2, 1, 3).reshape(E, P, DC * F),
        "w2": np.asarray(L0_ffn_w2).reshape(E, FC, P, D).transpose(0, 2, 1, 3).reshape(E, P, FC * D),
        "b12": np.concatenate([np.asarray(L0_ffn_b1), np.asarray(L0_ffn_b2)], axis=1),
        "consts": build_constants(),
    }
    arrays = {name: np.ascontiguousarray(a) for name, a in arrays.items()}
    nc = bacc.Bacc("TRN2", target_bir_lowering=False, num_devices=1)
    aps = [nc.dram_tensor(name, a.shape, mybir.dt.from_np(a.dtype), kind="ExternalInput").ap()
           for name, a in arrays.items()]
    out = nc.dram_tensor("out", (B, P, D), F32, kind="ExternalOutput").ap()
    flamingo_kernel(nc, *aps, out)
    r = run_bass_kernel_spmd(nc, [arrays], core_ids=[0])
    return r.results[0]["out"]
```

```python
from contextlib import ExitStack

import numpy as np
import concourse.bass as bass
from concourse import mybir

P = 128
B = 32
D = 256
DC = D // P
H = 16
DH = D // H
HQ = 4
QUADS = H // HQ
VP = 3
VW = VP * DH + 1
E = 14
F = 512
FC = F // P
TOK = B * P
REGION = TOK + P
SLOTS = (TOK - E) // P + E
R = 5
IDLE_ROWS = (SLOTS - TOK // P) * P
ROW = 2 * D
NEG = -1.0e9
EPS = 1e-5
NO_TOKEN = TOK
NAMES = E * REGION + IDLE_ROWS
LOGIT = D
RANK = LOGIT + 16

F32 = mybir.dt.float32
BF16 = mybir.dt.bfloat16
F16 = mybir.dt.float16
I32 = mybir.dt.int32
ALU = mybir.AluOpType
ACT = mybir.ActivationFunctionType
AX_X = mybir.AxisListType.X

CONST_COLS = {}


def build_constants():
    p = np.arange(P)[:, None]
    j = np.arange(P)[None, :]
    e = np.arange(E)[None, :]
    blocks = {
        "ident": (p == j),
        "causal": np.where(j > p, NEG, 0.0),
        "before": (p < j),
        "headmask": (p // DH) % HQ == np.arange(HQ)[None, :],
        "first": np.broadcast_to(16.0 - e, (P, E)),
        "region": np.broadcast_to(REGION * e, (P, E)),
        "slot": np.broadcast_to(np.arange(SLOTS)[None, :], (P, SLOTS)),
        "tile": np.broadcast_to(P * np.arange(B)[None, :], (P, B)),
        "select": (p % 32 == e) & (p < 96),
        "token": P * np.arange(B)[None, :] + p,
    }
    at = 0
    for name, block in blocks.items():
        CONST_COLS[name] = (at, at + block.shape[1])
        at += block.shape[1]
    return np.concatenate([np.asarray(b, dtype=np.float32) for b in blocks.values()], axis=1)


class Batch:

    def __init__(self, i, k):
        self.i, self.k = i, k
        self.n = i * 4 + k
        self.slot = k % 4
        self.par = k % 2
        self.round = i + k // 4
        self.static = isinstance(i, int)

    def ok(self, last=B - 1):
        return not self.static or 0 <= self.n <= last

    def back(self, k):
        return Batch(self.i, self.k - k)


def wait(eng, sem, value):
    if isinstance(value, int) and value <= 0:
        return
    eng.wait_ge(sem, value)


def run_steps(eng, step, deepest=7):
    first = -(-deepest // 4)
    for t in range(4 * first):
        step(Batch(0, t))
    with eng.Fori(first, B // 4) as i:
        for j in range(4):
            step(Batch(i, j))
    for t in range(B, B + deepest):
        step(Batch(B // 4, t - B))


def flamingo_kernel(nc, x, ctxt, gates, wq, wk, wv, wd, bqk, bv, bd, rw, w1, w2, b12, consts, out):
    token_rows = nc.dram_tensor("token_rows", [TOK + P, ROW], F32, kind="Internal").ap()
    token_names = nc.dram_tensor("token_names", [NAMES, 2], I32, kind="Internal").ap()
    x_view = x.rearrange("b s d -> s b d")
    out_rows = out.rearrange("b s d -> (b s) d")

    with ExitStack() as ctx:
        def sb(name, shape, dt=F32):
            return ctx.enter_context(nc.sbuf_tensor(name, shape, dt))

        def sem(name):
            return ctx.enter_context(nc.semaphore(name))

        W1 = sb("W1", [P, E, DC, F])
        W2 = sb("W2", [P, E, FC, D])
        C = sb("C", [P, consts.shape[1]])

        def const(name):
            a, b = CONST_COLS[name]
            return C[:, a:b]

        ident = const("ident")
        ident_bf = sb("ident_bf", [P, P], BF16)
        causal_bf = sb("causal_bf", [P, HQ, P], BF16)
        before_bf = sb("before_bf", [P, P], BF16)
        ones_bf = sb("ones_bf", [P, P], BF16)
        select_bf = sb("select_bf", [P, E, P], BF16)
        bias_parts = sb("bias_parts", [P, F + D], BF16)
        rows = sb("rows", [P, 4, ROW])
        gate_raw = sb("gate_raw", [P, 2])
        gate = sb("gate", [P, 2])
        half = sb("half", [P, 1])
        logits = sb("logits", [P, 4, E])
        onehot = sb("onehot", [P, 2, E], BF16)
        pair_seen = sb("pair_seen", [P, E], BF16)
        seen = sb("seen", [P, E], BF16)
        route_max = sb("route_max", [P, 2])
        route_eq = sb("route_eq", [P, 2, E])
        route_order = sb("route_order", [P, 2, E])
        route_pick = sb("route_pick", [P, 2])
        shifted = sb("shifted", [P, 2, E])
        exp_logits = sb("exp_logits", [P, 2, E])
        exp_sum = sb("exp_sum", [P, 2])
        exp_inv = sb("exp_inv", [P, 2])
        rank_at = sb("rank_at", [P, 2, E])
        pos_f = sb("pos_f", [P, 2])
        pos = sb("pos", [P, 4], I32)
        name = sb("name", [P, 4, 2], I32)
        stats = sb("stats", [P, 4, 6])
        moments = sb("moments", [P, 4, 2])
        rstd = sb("rstd", [P, 4, 2])
        stats2 = sb("stats2", [P, 4, 6])
        moments2 = sb("moments2", [P, 4, 2])
        rstd2 = sb("rstd2", [P, 4, 2])
        negmax = sb("negmax", [P, 2, H])
        rsum = sb("rsum", [P, H])

        ARENA = 14900
        arena = sb("arena", [P, ARENA])
        taken = [0]

        def part(n):
            taken[0] += n
            assert taken[0] <= ARENA, taken
            return arena[:, taken[0] - n:taken[0]]

        wq_sb = part(DC * D).rearrange("p (c n) -> p c n", c=DC)
        wk_sb = part(DC * D).rearrange("p (c n) -> p c n", c=DC)
        wv_sb = part(DC * D).rearrange("p (c n) -> p c n", c=DC)
        wd_sb = part(DC * D).rearrange("p (c n) -> p c n", c=DC)
        rw_sb = part(DC * E).rearrange("p (c n) -> p c n", c=DC)
        bqk_sb = part(2 * DC)
        bv_sb = part(DC)
        resid_bias = part(D)
        x_in = part(4 * D).rearrange("p (r d) -> p r d", r=4)
        c_in = part(4 * D).rearrange("p (r c s) -> p r c s", r=4, c=DC)
        x_biased = part(4 * D).rearrange("p (r d) -> p r d", r=4)
        xn = part(2 * D).rearrange("p (r d) -> p r d", r=2)
        xh_t = part(2 * 2 * D).rearrange("p (r c s) -> p r c s", r=2, c=4)
        q_t = part(2 * D).rearrange("p (r c s) -> p r c s", r=2, c=DC)
        k_t = part(D).rearrange("p (c s) -> p c s", c=DC)
        k_masked = part(2 * DC * HQ * P).rearrange("p (r c v s) -> p r c v s", r=2, c=DC, v=HQ)
        v_raw = part(D)
        v_rest = part(D)
        values = part(H * VW).bitcast(BF16).rearrange("p (r h w) -> p r h w", r=2, h=H)
        probs0 = taken[0]
        probs = part(QUADS * HQ * P).rearrange("p (q v k) -> p q v k", q=QUADS, v=HQ)
        probs_t = part(2 * HQ * P).bitcast(F16).rearrange("p (r o v s) -> p r o v s", r=2, o=2, v=HQ)
        attn_raw = part(D)
        attn = part(D)
        attn_t = part(D)
        bias_in = arena[:, probs0:probs0 + F + D]
        bias_rest = arena[:, probs0 + F + D:probs0 + 2 * (F + D)]
        bd_rep = attn_t
        bv_rep = x_biased[:, 3, :].rearrange("p (c s) -> p c s", c=DC)
        bias_mid = k_masked.rearrange("p r c v s -> p (r c v s)")[:, 0:(F + D) // 2].bitcast(BF16)

        taken[0] = 0
        g_rows = part(R * ROW).rearrange("p (r n) -> p r n", r=R)
        g_xt = part(R * D).rearrange("p (r c s) -> p r c s", r=R, c=DC)
        hid = part(R * F).rearrange("p (r n) -> p r n", r=R)
        hid_t = part(R * F).rearrange("p (r c s) -> p r c s", r=R, c=FC)
        g_out = part(R * D).rearrange("p (r n) -> p r n", r=R)
        g_name = part(R * 2).bitcast(I32).rearrange("p (r o) -> p r o", o=2)
        fetch_idx = part(R).bitcast(I32)
        slot_expert = part(SLOTS).bitcast(I32)
        slot_rows = part(SLOTS).bitcast(I32)
        slot_names = part(SLOTS * 2).bitcast(I32).rearrange("p (s o) -> p s o", o=2)
        t_a = part(SLOTS * E).rearrange("p (s e) -> p s e", s=SLOTS)
        t_b = part(SLOTS * E).rearrange("p (s e) -> p s e", s=SLOTS)
        t_cmp = part(E * B).rearrange("p (e j) -> p e j", e=E)
        t_cnt = part(E)
        t_tiles = part(E)
        t_cum = part(E)
        t_one = part(E)
        t_e = part(SLOTS)
        t_c = part(SLOTS)
        t_r = part(SLOTS)

        bank = [ctx.enter_context(nc.psum_tensor(f"bank{k}", [P, 512], F32)) for k in range(8)]

        hid_bank = [bank[k] for k in (0, 1, 2, 6, 7)]

        small_loaded = sem("small_loaded")
        bias_loaded = sem("bias_loaded")
        consts_loaded = sem("consts_loaded")
        attn_w_loaded = sem("attn_w_loaded")
        experts_loaded = sem("experts_loaded")
        x_loaded = [sem(f"x_loaded{r}") for r in range(4)]
        c_loaded = [sem(f"c_loaded{r}") for r in range(4)]
        idle_written = sem("idle_written")
        setup_pool = sem("setup_pool")
        bias_zeroed = sem("bias_zeroed")
        bias_step = sem("bias_step")
        tanh_done = sem("tanh_done")
        consts_cast = sem("consts_cast")
        bv_spread = sem("bv_spread")
        out_bias_done = sem("out_bias_done")
        resid_bias_ready = sem("resid_bias_ready")

        stats_done = sem("stats_done")
        moments_ready = sem("moments_ready")
        rstd_step = sem("rstd_step")
        xn_ready = sem("xn_ready")
        x_used = sem("x_used")
        xh_transposed = sem("xh_transposed")
        xh_ready = sem("xh_ready")
        qk_done = sem("qk_done")
        k_masked_ready = sem("k_masked_ready")
        v_done = sem("v_done")
        v_raw_ready = sem("v_raw_ready")
        v_split_step = sem("v_split_step")
        values_ready = sem("values_ready")
        probs_high_ready = sem("probs_high_ready")
        rstd_ready = sem("rstd_ready")
        rstd2_ready = sem("rstd2_ready")
        av_half_read = sem("av_half_read")
        scores_ready = sem("scores_ready")
        max_ready = sem("max_ready")
        probs_ready = sem("probs_ready")
        q_ready = sem("q_ready")
        k_ready = sem("k_ready")
        probs_transposed = sem("probs_transposed")
        probs_t_ready = sem("probs_t_ready")
        av_done = sem("av_done")
        rsum_ready = sem("rsum_ready")
        token_written = sem("token_written")
        weight_ready = sem("weight_ready")
        wd_scaled = sem("wd_scaled")
        attn_ready = sem("attn_ready")
        mixed_done = sem("mixed_done")
        mixed_ready = sem("mixed_ready")
        dense_done = sem("dense_done")
        x2_ready = sem("x2_ready")
        stats2_done = sem("stats2_done")
        moments2_ready = sem("moments2_ready")
        rstd2_step = sem("rstd2_step")
        h_ready = sem("h_ready")
        route_step = sem("route_step")
        shifted_ready = sem("shifted_ready")
        onehot_ready = sem("onehot_ready")
        exp_logits_ready = sem("exp_logits_ready")
        pos_summed = sem("pos_summed")
        seen_ready = sem("seen_ready")
        pos_ready = sem("pos_ready")
        row_stored = [sem(f"row_stored{r}") for r in range(4)]
        name_stored = [sem(f"name_stored{r}") for r in range(4)]
        names_loaded = [sem(f"names_loaded{r}") for r in range(R)]

        load_waits = sem("load_waits")
        pool_waits = sem("pool_waits")
        vector_waits = sem("vector_waits")
        counts_done = sem("counts_done")
        table_step = sem("table_step")
        tables_ready = sem("tables_ready")
        rows_fetched = [sem(f"rows_fetched{r}") for r in range(R)]
        fetch_named = sem("fetch_named")
        gx_transposed = sem("gx_transposed")
        gx_ready = sem("gx_ready")
        hid_done = sem("hid_done")
        hid_ready = sem("hid_ready")
        hid_transposed = sem("hid_transposed")
        hid_t_ready = sem("hid_t_ready")
        y_done = sem("y_done")
        out_ready = sem("out_ready")
        idx_ready = sem("idx_ready")
        out_stored = [sem(f"out_stored{r}") for r in range(R)]

        block = ctx.enter_context(nc.Block())

        @block.sync
        def _(sp):
            sp.dma_start(C[:, :], consts).then_inc(consts_loaded, 16)

            def hold(sem_, value):
                wait(sp, sem_, value)
                if not isinstance(value, int):
                    sp.sem_inc(load_waits, 1)

            def load(b):
                hold(x_used, b.n - 3)
                hold(xn_ready, b.n - 3)
                sp.dma_start(x_in[:, b.slot, :], x_view[:, bass.ds(b.n, 1), :]
                             .rearrange("s b d -> s (b d)")).then_inc(x_loaded[b.slot], 16)
                hold(v_done, b.n - 3)
                sp.dma_start(c_in[:, b.slot, :, :].rearrange("p c s -> p (c s)"),
                             ctxt[:, bass.ds(b.n, 1), :].rearrange("p b n -> p (b n)")
                             ).then_inc(c_loaded[b.slot], 16)

            def store(b):
                hold(h_ready, b.n + 1)
                sp.dma_start(token_rows[bass.ds(b.n * P, P), :], rows[:, b.slot, :]).then_inc(row_stored[b.slot], 16)

            def step(t):
                b = t.back(6)
                if b.ok():
                    store(b)
                if t.ok():
                    load(t)
                if t.static and t.n == 0:
                    for dst, src in ((wq_sb, wq), (wk_sb, wk), (wv_sb, wv), (wd_sb, wd), (rw_sb, rw)):
                        sp.dma_start(dst, src).then_inc(attn_w_loaded, 16)

            run_steps(sp, step)

            for r in range(4):
                hold(name_stored[r], 16 * (B // 4) + 16)
            hold(tables_ready, 1)

            def load_names(r, s):
                row = sp.value_load(slot_rows[0:1, bass.ds(s, 1)], min_val=0, max_val=NAMES - P)
                sp.dma_start(slot_names[:, bass.ds(s, 1), :].rearrange("p s o -> p (s o)"), token_names[bass.ds(row, P), :]
                             ).then_inc(names_loaded[r], 16)

            for k in range(R):
                load_names(k, k)
            with sp.Fori(1, SLOTS // R) as i:
                for k in range(R):
                    hold(names_loaded[k], i * 16)
                    load_names(k, i * R + k)

        @block.gpsimd
        def _(pool):
            done = [0]

            def link(ins):
                done[0] += 1
                ins.then_inc(setup_pool, 1)
                pool.wait_ge(setup_pool, done[0])

            pool.memset(bias_in, 0.0).then_inc(bias_zeroed, 1)
            pool.memset(half[:, :], -0.5)
            pool.memset(values, 1.0)
            pool.memset(seen[:, :], 0.0)
            pool.memset(ones_bf[:, :], 1.0)
            link(pool.memset(rows[:, 3, :], 0.0))
            pool.dma_start(token_rows[TOK:TOK + P, :], rows[:, 3, :]).then_inc(idle_written, 16)
            no_names = k_masked.rearrange("p r c v s -> p (r c v s)").bitcast(I32)[:, F + D:F + D + NAMES // P * 2]
            link(pool.memset(no_names, NO_TOKEN))
            blank = token_names.rearrange("(p n) o -> p (n o)", p=P)
            for r in range(4):
                n = slice(r * NAMES // P // 2, (r + 1) * NAMES // P // 2)
                pool.dma_start(blank[:, n], no_names[:, n]).then_inc(name_stored[r], 16)
            pool.wait_ge(idle_written, 16)
            for r in range(4):
                pool.wait_ge(name_stored[r], 16)
            pool.wait_ge(consts_loaded, 16)
            pool.wait_ge(resid_bias_ready, 1)

            def hold(sem_, value):
                wait(pool, sem_, value)
                if not isinstance(value, int):
                    pool.sem_inc(pool_waits, 1)

            def inverse_std(b, var, rs, counter, done_):
                pool.tensor_scalar(rs[:, b.slot, 0:1], var, EPS, None, ALU.add).then_inc(counter, 1)
                hold(counter, b.n + 1)
                pool.tensor_tensor(rs[:, b.slot, 1:2], rs[:, b.slot, 0:1], half[:, :], ALU.pow).then_inc(done_, 1)

            def step(t):
                a, a1, a2, d, g = t, t.back(1), t.back(2), t.back(4), t.back(7)
                if a2.ok():
                    def part_of(k):
                        return values[:, a2.par, :, k * DH:(k + 1) * DH]

                    raw, rest = (w.rearrange("p (h w) -> p h w", h=H) for w in (v_raw, v_rest))
                    hold(v_raw_ready, a2.n + 1)
                    hold(av_done, a2.n * 4 - 4)
                    pool.tensor_copy(part_of(0), raw).then_inc(v_split_step, 1)
                if d.ok():
                    hold(moments2_ready, d.n + 1)
                    inverse_std(d, moments2[:, d.slot, 1:2], rstd2, rstd2_step, rstd2_ready)
                if a2.ok():
                    hold(v_split_step, a2.n * 3 + 1)
                    pool.tensor_tensor(rest, raw, part_of(0), ALU.subtract).then_inc(v_split_step, 1)
                    hold(v_split_step, a2.n * 3 + 2)
                    pool.tensor_copy(part_of(1), rest).then_inc(v_split_step, 1)
                    hold(v_split_step, a2.n * 3 + 3)
                    pool.tensor_tensor(part_of(2), rest, part_of(1), ALU.subtract).then_inc(values_ready, 1)
                if a.ok():
                    hold(x_loaded[a.slot], (a.round + 1) * 16)
                    hold(x2_ready, a.n - 3)
                    pool.tensor_tensor(x_biased[:, a.slot, :], x_in[:, a.slot, :], resid_bias,
                                       ALU.add).then_inc(x_used, 1)
                if g.ok() and g.par == 1:
                    for b in (g.back(1), g):
                        hold(name_stored[b.slot], b.round * 16 + 16)
                        pool.tensor_copy(name[:, b.slot, 0:1],
                                         const("token")[:, bass.ds(b.n, 1)]).then_inc(token_written, 1)
                    hold(token_written, g.n + 1)
                    hold(pos_ready, g.n + 1)
                    hold(weight_ready, g.n + 1)
                    for b in (g.back(1), g):
                        pool.indirect_dma_start(
                            out=token_names, out_offset=bass.IndirectOffsetOnAxis(ap=pos[:, b.slot:b.slot + 1], axis=0),
                            in_=name[:, b.slot, :], in_offset=None).then_inc(name_stored[b.slot], 16)
                if a.ok():
                    hold(moments_ready, a.n + 1)
                    inverse_std(a, moments[:, a.slot, 1:2], rstd, rstd_step, rstd_ready)
                if a1.ok():
                    hold(k_ready, a1.n + 1)
                    hold(scores_ready, a1.n * 4 - 4)
                    for ch in range(DC):
                        ins = pool.tensor_tensor(
                            k_masked[:, a1.par, ch, :, :],
                            k_t[:, ch, :].rearrange("p (o s) -> p o s", o=1).to_broadcast([P, HQ, P]),
                            const("headmask").rearrange("p (v o) -> p v o", o=1).to_broadcast([P, HQ, P]),
                            ALU.mult)
                    ins.then_inc(k_masked_ready, 1)

            run_steps(pool, step)

            for r in range(4):
                hold(row_stored[r], 16 * (B // 4))
            hold(tables_ready, 1)

            def fetch(r, s, rnd):
                hold(names_loaded[r], rnd * 16 + 16)
                pool.tensor_copy(fetch_idx[:, r:r + 1], slot_names[:, bass.ds(s, 1), 0]).then_inc(fetch_named, 1)
                hold(fetch_named, s + 1)
                pool.indirect_dma_start(
                    out=g_rows[:, r, :], out_offset=None, in_=token_rows,
                    in_offset=bass.IndirectOffsetOnAxis(ap=fetch_idx[:, r:r + 1], axis=0)
                ).then_inc(rows_fetched[r], 16)

            def store(r, s):
                hold(idx_ready, s + 1)
                hold(out_ready, s + 1)
                pool.indirect_dma_start(
                    out=out_rows, out_offset=bass.IndirectOffsetOnAxis(ap=g_name[:, r, 0:1], axis=0),
                    in_=g_out[:, r, :], in_offset=None, bounds_check=TOK - 1, oob_is_err=False
                ).then_inc(out_stored[r], 16)

            for k in range(R):
                fetch(k, k, 0)
            with pool.Fori(0, SLOTS // R - 1) as i:
                for k in range(R):
                    store(k, i * R + k)
                    fetch(k, i * R + (k + R), i + 1)
            for k in range(R):
                store(k, SLOTS - R + k)
            for k in range(R):
                pool.wait_ge(out_stored[k], 16 * (SLOTS // R))

        @block.scalar
        def _(act):
            act.dma_start(gate_raw[:, :], gates.to_broadcast([P, 2])).then_inc(small_loaded, 16)
            act.dma_start(bqk_sb, bqk).then_inc(small_loaded, 16)
            act.dma_start(bv_sb, bv).then_inc(small_loaded, 16)
            act.dma_start(bd_rep, bd.to_broadcast([P, D])).then_inc(small_loaded, 16)
            act.wait_ge(bias_zeroed, 1)
            for g in range(3):
                act.dma_start(bias_in[32 * g:32 * g + E, :], b12).then_inc(bias_loaded, 16)
            act.wait_ge(small_loaded, 64)
            act.activation(gate[:, :], gate_raw[:, :], ACT.Tanh).then_inc(tanh_done, 1)
            for e in range(E):
                act.dma_start(W1[:, e, :, :].rearrange("p c n -> p (c n)"), w1[e]).then_inc(experts_loaded, 16)
                act.dma_start(W2[:, e, :, :].rearrange("p c n -> p (c n)"), w2[e]).then_inc(experts_loaded, 16)

            def step(t):
                a1, b, c, d, e = (t.back(k) for k in range(1, 6))

                def exponentials(q):
                    act.wait_ge(max_ready, b.n * 4 + (q + 1))
                    wait(act, probs_transposed, b.n * 4 + (q - 3))
                    for v in range(HQ):
                        h = q * HQ + v
                        ins = act.activation(probs[:, q, v, :], bank[q][:, v * P:(v + 1) * P], ACT.Exp,
                                             bias=negmax[:, b.par, h:h + 1])
                    ins.then_inc(probs_ready, 1)

                def high_probs(q):
                    act.wait_ge(probs_transposed, b.n * 4 + (q + 1))
                    wait(act, av_done, b.n * 4 + (q - 1))
                    act.activation(probs_t[:, q % 2, 0, :, :].rearrange("p v s -> p (v s)"),
                                   bank[5 - q % 2][:, :], ACT.Copy).then_inc(probs_high_ready, 1)

                if b.ok():
                    for q in range(3):
                        exponentials(q)
                if a1.ok() or d.ok():
                    lo, hi = (0 if a1.ok() else DC), (4 if d.ok() else DC)
                    act.wait_ge(xh_transposed, t.n)
                    if t.back(6).ok() or not t.static:
                        act.wait_ge(mixed_done, t.n - 3)
                    else:
                        wait(act, qk_done, a1.n - 1)
                    act.activation(xh_t[:, t.par, lo:hi, :].rearrange("p c s -> p (c s)"),
                                   bank[6][:, lo * P:hi * P], ACT.Copy).then_inc(xh_ready, 1)
                if b.ok():
                    high_probs(0)
                    high_probs(1)
                    exponentials(3)
                if a1.ok():
                    act.wait_ge(qk_done, a1.n + 1)
                    wait(act, k_masked_ready, a1.n)
                    for ch in range(DC):
                        ins = act.activation(k_t[:, ch, :], bank[6][:, (DC + ch) * P:(DC + ch + 1) * P],
                                             ACT.Identity, bias=bqk_sb[:, DC + ch:DC + ch + 1])
                    ins.then_inc(k_ready, 1)
                if b.ok():
                    high_probs(2)
                if e.ok() and e.par == 1:
                    act.wait_ge(shifted_ready, e.n + 1)
                    act.activation(exp_logits[:, :, :], shifted[:, :, :], ACT.Exp).then_inc(exp_logits_ready, 2)
                if b.ok():
                    high_probs(3)
                if a1.ok():
                    act.wait_ge(v_done, a1.n + 1)
                    if c.ok():
                        act.wait_ge(dense_done, c.n + 1)
                    wait(act, values_ready, a1.n)
                    act.activation(v_raw, bank[6][:, 0:D], ACT.Copy).then_inc(v_raw_ready, 1)

            run_steps(act, step)

            def gelu(k, s):
                act.wait_ge(hid_done, s + 1)
                act.activation(hid[:, k, :], hid_bank[k][:, :], ACT.Gelu).then_inc(hid_ready, 1)

            with act.Fori(0, SLOTS // R) as i:
                for k in range(R):
                    gelu(k, i * R + k)

        @block.vector
        def _(dve):
            dve.wait_ge(consts_loaded, 16)
            dve.tensor_copy(ident_bf[:, :], ident)
            dve.tensor_copy(causal_bf[:, :, :], const("causal").rearrange("p (o k) -> p o k", o=1)
                            .to_broadcast([P, HQ, P]))
            dve.tensor_copy(before_bf[:, :], const("before"))
            dve.tensor_copy(select_bf[:, :, :], const("select").rearrange("p (e o) -> p e o", o=1)
                            .to_broadcast([P, E, P])).then_inc(consts_cast, 1)
            dve.wait_ge(small_loaded, 64)
            dve.tensor_copy(bv_rep, bv_sb.rearrange("p (c o) -> p c o", o=1).to_broadcast([P, DC, P])
                            ).then_inc(bv_spread, 1)
            split = [0]

            def next_part(ins):
                split[0] += 1
                ins.then_inc(bias_step, 1)
                dve.wait_ge(bias_step, split[0])

            dve.wait_ge(bias_loaded, 48)
            next_part(dve.tensor_copy(bias_parts[:, :], bias_in))
            next_part(dve.tensor_tensor(bias_rest, bias_in, bias_parts[:, :], ALU.subtract))
            next_part(dve.tensor_copy(bias_mid, bias_rest))
            next_part(dve.tensor_copy(bias_parts[32:64, :], bias_mid[32:64, :]))
            next_part(dve.tensor_tensor(bias_rest, bias_rest, bias_mid, ALU.subtract))
            next_part(dve.tensor_copy(bias_parts[64:96, :], bias_rest[64:96, :]))
            dve.wait_ge(out_bias_done, 1)
            dve.tensor_tensor(resid_bias, bank[7][:, 0:D], bd_rep, ALU.add).then_inc(bv_spread, 1)
            dve.wait_ge(bv_spread, 2)
            dve.wait_ge(tanh_done, 1)
            dve.tensor_scalar(resid_bias, resid_bias, gate[:, 0:1], None, ALU.mult).then_inc(resid_bias_ready, 1)
            dve.tensor_scalar(wd_sb, wd_sb, gate[:, 0:1], None, ALU.mult).then_inc(wd_scaled, 1)

            def step(t):
                a, a1, b, c, d, e, f = t, t.back(1), t.back(2), t.back(3), t.back(4), t.back(5), t.back(6)
                routes = e.ok() and e.par == 1

                def maxima(q):
                    dve.wait_ge(scores_ready, b.n * 4 + (q + 1))
                    dve.tensor_reduce(negmax[:, b.par, q * HQ:(q + 1) * HQ],
                                      bank[q][:, :].rearrange("p (v k) -> p v k", v=HQ),
                                      axis=AX_X, op=ALU.max, negate=True).then_inc(max_ready, 1)

                def transposed_probs(q):
                    dve.wait_ge(probs_high_ready, b.n * 4 + (q + 1))
                    high, low = (probs_t[:, q % 2, o, :, :].rearrange("p v s -> p (v s)") for o in range(2))
                    dve.tensor_tensor(low, bank[5 - q % 2][:, :], high, ALU.subtract).then_inc(probs_t_ready, 1)

                def half_attention(n, hf):
                    raw = attn_raw.rearrange("p (h w) -> p h w", h=H)[:, 8 * hf:8 * hf + 8, :]
                    av = bank[7][:, 0:8 * VW].rearrange("p (h w) -> p h w", h=8)
                    dve.wait_ge(av_done, n.n * 4 + (2 * hf + 2))
                    if hf == 0:
                        wait(dve, mixed_done, n.n)
                    dve.reciprocal(rsum[:, 8 * hf:8 * hf + 8], av[:, :, VP * DH]).then_inc(rsum_ready, 1)
                    dve.tensor_reduce(raw, av[:, :, 0:VP * DH].rearrange("p h (k w) -> p h w k", k=VP),
                                      axis=AX_X, op=ALU.add).then_inc(av_half_read, 1)
                    dve.wait_ge(rsum_ready, n.n * 2 + (hf + 1))
                    dve.wait_ge(av_half_read, n.n * 2 + (hf + 1))
                    ins = dve.tensor_tensor(attn.rearrange("p (h w) -> p h w", h=H)[:, 8 * hf:8 * hf + 8, :], raw,
                                            rsum[:, 8 * hf:8 * hf + 8].rearrange("p (h o) -> p h o", o=1)
                                            .to_broadcast([P, 8, DH]), ALU.mult)
                    if hf == 1:
                        ins.then_inc(attn_ready, 1)

                def normed(n, dst, src, mom, rs, ready, signal):
                    dve.wait_ge(ready, n.n + 1)
                    dve.tensor_scalar(dst, src, mom[:, n.slot, 0:1], rs[:, n.slot, 1:2],
                                      ALU.subtract, ALU.mult).then_inc(signal, 1)

                if a1.ok():
                    wait(dve, xh_transposed, a1.n - 1)
                    normed(a1, xn[:, a1.par, :], x_in[:, a1.slot, :], moments, rstd, rstd_ready, xn_ready)
                if d.ok():
                    dve.wait_ge(dense_done, d.n + 1)
                    dve.wait_ge(v_raw_ready, min(t.n - 1, B) if t.static else t.n - 1)
                    dve.wait_ge(x_used, d.n + 1)
                    wait(dve, row_stored[d.slot], d.round * 16)
                    dve.tensor_tensor(rows[:, d.slot, D:2 * D], bank[6][:, D:2 * D], x_biased[:, d.slot, :],
                                      ALU.add).then_inc(x2_ready, 1)
                    dve.wait_ge(x2_ready, d.n + 1)
                    dve.bn_stats(stats2[:, d.slot, :], rows[:, d.slot, D:2 * D]).then_inc(stats2_done, 1)
                if b.ok():
                    maxima(0)
                if d.ok():
                    dve.wait_ge(stats2_done, d.n + 1)
                    dve.sem_inc(vector_waits, 1)
                    dve.bn_aggr(moments2[:, d.slot, :], stats2[:, d.slot, :]).then_inc(moments2_ready, 1)
                if b.ok():
                    maxima(1)
                if c.ok():
                    half_attention(c, 1)
                if d.ok():
                    normed(d, rows[:, d.slot, 0:D], rows[:, d.slot, D:2 * D], moments2, rstd2, rstd2_ready, h_ready)
                if b.ok():
                    maxima(2)
                    maxima(3)
                if c.ok() or e.ok() or (f.ok() and f.par == 1):
                    dve.wait_ge(mixed_done, t.n - 2)
                    if e.ok():
                        ins = dve.tensor_copy(logits[:, e.slot, :], bank[4][:, LOGIT:LOGIT + E])
                    if f.ok() and f.par == 1:
                        dve.wait_ge(onehot_ready, f.n + 1)
                        ins = dve.tensor_tensor(rank_at[:, :, :],
                                                bank[4][:, RANK:RANK + 2 * E].rearrange("p (r e) -> p r e", r=2),
                                                const("region").rearrange("p (o e) -> p o e", o=1)
                                                .to_broadcast([P, 2, E]), ALU.add)
                    if c.ok():
                        wait(dve, dense_done, c.n)
                        ins = dve.tensor_copy(attn_t, bank[4][:, 0:D])
                    ins.then_inc(mixed_ready, 1)
                if routes:
                    pair = logits[:, e.slot - 1:e.slot + 1, :]
                    base = (e.n - 1) * 4
                    dve.wait_ge(mixed_ready, t.n - 2)
                    wait(dve, mixed_done, t.n - 2)
                    dve.tensor_reduce(route_max[:, :], pair, axis=AX_X, op=ALU.max).then_inc(route_step, 1)
                    dve.wait_ge(route_step, base + 1)
                    top = route_max[:, :].rearrange("p (r o) -> p r o", o=1).to_broadcast([P, 2, E])
                    dve.tensor_tensor(route_eq[:, :, :], pair, top, ALU.is_equal).then_inc(route_step, 1)
                    dve.tensor_tensor(shifted[:, :, :], pair, top, ALU.subtract).then_inc(shifted_ready, 2)
                    dve.wait_ge(route_step, base + 2)
                    dve.tensor_tensor(route_order[:, :, :], route_eq[:, :, :],
                                      const("first").rearrange("p (o e) -> p o e", o=1).to_broadcast([P, 2, E]),
                                      ALU.mult).then_inc(route_step, 1)
                    dve.wait_ge(route_step, base + 3)
                    dve.tensor_reduce(route_pick[:, :], route_order[:, :, :], axis=AX_X,
                                      op=ALU.max).then_inc(route_step, 1)
                    dve.wait_ge(route_step, base + 4)
                    dve.tensor_tensor(onehot[:, :, :], route_order[:, :, :],
                                      route_pick[:, :].rearrange("p (r o) -> p r o", o=1).to_broadcast([P, 2, E]),
                                      ALU.is_equal).then_inc(onehot_ready, 2)
                if a.ok():
                    dve.wait_ge(x_loaded[a.slot], (a.round + 1) * 16)
                    dve.bn_stats(stats[:, a.slot, :], x_in[:, a.slot, :]).then_inc(stats_done, 1)
                    dve.wait_ge(stats_done, a.n + 1)
                    dve.sem_inc(vector_waits, 1)
                    dve.bn_aggr(moments[:, a.slot, :], stats[:, a.slot, :]).then_inc(moments_ready, 1)
                if b.ok():
                    transposed_probs(0)
                    transposed_probs(1)
                if a1.ok():
                    dve.wait_ge(k_ready, a1.n + 1)
                    wait(dve, scores_ready, a1.n * 4 - 4)
                    for ch in range(DC):
                        ins = dve.tensor_scalar(q_t[:, a1.par, ch, :], bank[6][:, ch * P:(ch + 1) * P],
                                                bqk_sb[:, ch:ch + 1], float(DH) ** -0.5, ALU.add, ALU.mult)
                    ins.then_inc(q_ready, 1)
                if f.ok() and f.par == 1:
                    base = (f.n - 1) * 4
                    dve.wait_ge(exp_logits_ready, f.n + 1)
                    dve.tensor_reduce(exp_sum[:, :], exp_logits[:, :, :], axis=AX_X,
                                      op=ALU.add).then_inc(route_step, 1)
                    dve.tensor_tensor(pair_seen[:, :], onehot[:, 0, :], onehot[:, 1, :],
                                      ALU.add).then_inc(route_step, 1)
                    dve.wait_ge(mixed_ready, t.n - 2)
                    dve.tensor_tensor(rank_at[:, :, :], rank_at[:, :, :], onehot[:, :, :],
                                      ALU.mult).then_inc(route_step, 1)
                    dve.wait_ge(route_step, base + 5)
                    dve.reciprocal(exp_inv[:, :], exp_sum[:, :]).then_inc(route_step, 1)
                    dve.wait_ge(route_step, base + 6)
                    dve.tensor_tensor(seen[:, :], seen[:, :], pair_seen[:, :], ALU.add).then_inc(seen_ready, 2)
                    dve.wait_ge(route_step, base + 7)
                    dve.tensor_reduce(pos_f[:, :], rank_at[:, :, :], axis=AX_X,
                                      op=ALU.add).then_inc(pos_summed, 2)
                    dve.wait_ge(route_step, base + 8)
                    for n in (f.back(1), f):
                        wait(dve, name_stored[n.slot], n.round * 16 + 16)
                    dve.tensor_scalar(name[:, f.slot - 1:f.slot + 1, 1].bitcast(F32),
                                      exp_inv[:, :], gate[:, 1:2], None, ALU.mult).then_inc(weight_ready, 2)
                    dve.wait_ge(pos_summed, f.n + 1)
                    dve.tensor_copy(pos[:, f.slot - 1:f.slot + 1], pos_f[:, :]).then_inc(pos_ready, 2)
                if b.ok():
                    transposed_probs(2)
                    half_attention(b, 0)
                    transposed_probs(3)

            run_steps(dve, step)

            done = [0]

            def link(ins):
                done[0] += 1
                ins.then_inc(table_step, 1)
                dve.wait_ge(table_step, done[0])

            def over_e(ap, n):
                return ap.rearrange("p (s o) -> p s o", o=1).to_broadcast([P, n, E])

            def over_s(ap):
                return ap.rearrange("p (o e) -> p o e", o=1).to_broadcast([P, SLOTS, E])

            dve.wait_ge(counts_done, 1)
            dve.memset(t_one, 1.0)
            link(dve.tensor_copy(t_cnt, bank[7][:, 0:E]))
            link(dve.tensor_tensor(t_cmp, t_cnt.rearrange("p (e o) -> p e o", o=1).to_broadcast([P, E, B]),
                                   const("tile").rearrange("p (o j) -> p o j", o=1).to_broadcast([P, E, B]),
                                   ALU.is_gt))
            link(dve.tensor_reduce(t_tiles, t_cmp, axis=AX_X, op=ALU.add))
            link(dve.tensor_tensor_scan(t_cum, t_one, t_tiles, 0.0, ALU.mult, ALU.add))
            link(dve.tensor_tensor(t_a, over_s(t_cum), over_e(const("slot"), SLOTS), ALU.is_le))
            dve.tensor_reduce(t_e, t_a, axis=AX_X, op=ALU.add)
            link(dve.tensor_tensor(t_b, over_s(t_cum), t_a, ALU.mult))
            link(dve.tensor_reduce(t_c, t_b, axis=AX_X, op=ALU.max))
            link(dve.tensor_tensor(t_c, const("slot"), t_c, ALU.subtract))
            link(dve.tensor_scalar(t_c, t_c, float(P), None, ALU.mult))
            link(dve.tensor_scalar(t_r, t_e, float(REGION), None, ALU.mult))
            link(dve.tensor_tensor(t_r, t_r, t_c, ALU.add))
            dve.tensor_copy(slot_rows, t_r)
            link(dve.tensor_scalar(t_e, t_e, float(E - 1), None, ALU.min))
            dve.tensor_copy(slot_expert, t_e).then_inc(tables_ready, 1)

            def up(r, s):
                dve.wait_ge(gx_transposed, s + 1)
                dve.tensor_copy(g_xt[:, r, :, :].rearrange("p c s -> p (c s)"), bank[3][:, 0:D]).then_inc(gx_ready, 1)

            def down(r, s):
                dve.wait_ge(hid_transposed, s + 1)
                dve.tensor_copy(hid_t[:, r, :, :].rearrange("p c s -> p (c s)"), bank[4][:, :]).then_inc(hid_t_ready, 1)

            def result(r, s, rnd):
                wait(dve, out_stored[r], rnd * 16)
                dve.tensor_copy(g_name[:, r, :], slot_names[:, bass.ds(s, 1), :].rearrange("p s o -> p (s o)")
                                ).then_inc(idx_ready, 1)
                dve.wait_ge(idx_ready, s + 1)
                dve.wait_ge(y_done, s + 1)
                dve.scalar_tensor_tensor(g_out[:, r, :], bank[5][:, 0:D], g_name[:, r, 1:2].bitcast(F32),
                                         g_rows[:, r, D:2 * D], ALU.mult, ALU.add).then_inc(out_ready, 1)

            def slot(k, s, rnd, ahead=True):
                down(k, s)
                if ahead:
                    up((k + 2) % R, s + 2)
                result(k, s, rnd)

            up(0, 0)
            up(1, 1)
            for k in range(R):
                slot(k, k, 0)
            with dve.Fori(1, SLOTS // R - 1) as i:
                for k in range(R):
                    slot(k, i * R + k, i)
            for k in range(R):
                slot(k, SLOTS - R + k, SLOTS // R - 1, ahead=k + 2 < R)

        @block.tensor
        def _(pe):
            pe.wait_ge(attn_w_loaded, 16 * 5)
            pe.wait_ge(bv_spread, 1)
            for ch in range(DC):
                ins = pe.matmul(bank[7][:, 0:D], bv_rep[:, ch, :], wd_sb[:, ch, :], start=(ch == 0), stop=(ch == DC - 1))
            ins.then_inc(out_bias_done, 1)
            pe.wait_ge(resid_bias_ready, 1)
            pe.wait_ge(consts_cast, 1)
            pe.wait_ge(wd_scaled, 1)

            def step(t):
                a1, b, c, d, e, f = (t.back(k) for k in range(1, 7))

                def scores(ch):
                    for r in range(2):
                        q = 2 * ch + r
                        wait(pe, probs_ready, b.n * 4 + (q - 3))
                        pe.matmul(bank[q][:, :], ident_bf[:, :], causal_bf[:, :, :].rearrange("p v k -> p (v k)"),
                                  start=True, stop=False)
                    for r in range(2):
                        q = 2 * ch + r
                        g = slice(64 * r, 64 * r + 64)
                        pe.matmul(bank[q][:, :], q_t[g, b.par, ch, :],
                                  k_masked[g, b.par, ch, :, :].rearrange("p v k -> p (v k)"),
                                  start=False, stop=True).then_inc(scores_ready, 1)

                def transpose_probs(q):
                    pe.wait_ge(probs_ready, b.n * 4 + (q + 1))
                    for v in range(HQ):
                        ins = pe.transpose(bank[5 - q % 2][:, v * P:(v + 1) * P], probs[:, q, v, :], ident)
                    ins.then_inc(probs_transposed, 1)

                def attend(n, q):
                    pe.wait_ge(probs_t_ready, n.n * 4 + (q + 1))
                    for v in range(HQ):
                        h = q * HQ + v
                        at = (h % 8) * VW
                        for o in range(2):
                            ins = pe.matmul(bank[7][:, at:at + VW], probs_t[:, q % 2, o, v, :],
                                            values[:, n.par, h, :], start=(o == 0), stop=(o == 1))
                    ins.then_inc(av_done, 1)

                if b.ok():
                    pe.wait_ge(q_ready, b.n + 1)
                    pe.wait_ge(k_masked_ready, b.n + 1)
                    scores(0)
                if c.ok():
                    attend(c, 3)
                if b.ok():
                    scores(1)
                if c.ok():
                    pe.wait_ge(attn_ready, c.n + 1)
                    for ch in range(DC):
                        ins = pe.transpose(bank[4][:, ch * P:(ch + 1) * P], attn[:, ch * P:(ch + 1) * P], ident)
                if e.ok():
                    pe.wait_ge(xh_ready, t.n - 1)
                    if not c.ok():
                        pe.wait_ge(mixed_ready, t.n - 3)
                    for ch in range(DC):
                        ins = pe.matmul(bank[4][:, LOGIT:LOGIT + E], xh_t[:, 1 - t.par, DC + ch, :], rw_sb[:, ch, :],
                                        start=(ch == 0), stop=(ch == DC - 1))
                if f.ok() and f.par == 1:
                    pe.wait_ge(onehot_ready, f.n + 1)
                    wait(pe, seen_ready, f.n - 1)
                    at = bank[4][:, RANK:RANK + 2 * E]
                    pe.matmul(at, before_bf[:, :], onehot[:, :, :].rearrange("p r e -> p (r e)"),
                              start=True, stop=False)
                    pe.matmul(at[:, E:2 * E], ones_bf[:, :], onehot[:, 0, :], start=False, stop=False)
                    for r in range(2):
                        ins = pe.matmul(at[:, r * E:(r + 1) * E], ones_bf[:, :], seen[:, :],
                                        start=False, stop=(r == 1))
                if c.ok() or e.ok() or (f.ok() and f.par == 1):
                    ins.then_inc(mixed_done, 1)
                if a1.ok() or d.ok():
                    wait(pe, v_raw_ready, min(t.n - 1, B) if t.static else t.n - 1)
                    if d.ok():
                        pe.wait_ge(x2_ready, d.n + 1)
                    if a1.ok():
                        pe.wait_ge(xn_ready, a1.n + 1)
                        for ch in range(DC):
                            ins = pe.transpose(bank[6][:, ch * P:(ch + 1) * P], xn[:, a1.par, ch * P:(ch + 1) * P], ident)
                    if d.ok():
                        pe.wait_ge(h_ready, d.n + 1)
                        for ch in range(DC):
                            ins = pe.transpose(bank[6][:, (DC + ch) * P:(DC + ch + 1) * P],
                                               rows[:, d.slot, ch * P:(ch + 1) * P], ident)
                    ins.then_inc(xh_transposed, 1)
                if b.ok():
                    transpose_probs(0)
                if c.ok():
                    pe.wait_ge(mixed_ready, t.n - 2)
                if b.ok():
                    transpose_probs(1)
                if a1.ok():
                    pe.wait_ge(xh_ready, t.n)
                    pe.wait_ge(c_loaded[a1.slot], (a1.round + 1) * 16)
                    for k, w in ((1, wk_sb), (0, wq_sb)):
                        for half_ in range(DC):
                            at = (k * DC + half_) * P
                            for ch in range(DC):
                                src = xh_t[:, t.par, ch, :] if k == 0 else c_in[:, a1.slot, ch, :]
                                ins = pe.matmul(bank[6][:, at:at + P], w[:, ch, half_ * P:(half_ + 1) * P], src,
                                                start=(ch == 0), stop=(ch == DC - 1))
                    ins.then_inc(qk_done, 1)
                if b.ok():
                    pe.wait_ge(values_ready, b.n + 1)
                    attend(b, 0)
                    transpose_probs(2)
                    attend(b, 1)
                    transpose_probs(3)
                if a1.ok():
                    pe.wait_ge(q_ready, a1.n + 1)
                    for ch in range(DC):
                        ins = pe.matmul(bank[6][:, 0:D], c_in[:, a1.slot, ch, :], wv_sb[:, ch, :],
                                        start=(ch == 0), stop=(ch == DC - 1))
                    ins.then_inc(v_done, 1)
                elif d.ok():
                    pe.wait_ge(xh_ready, t.n)
                if c.ok():
                    for ch in range(DC):
                        ins = pe.matmul(bank[6][:, D:2 * D], attn_t[:, ch * P:(ch + 1) * P], wd_sb[:, ch, :],
                                        start=(ch == 0), stop=(ch == DC - 1))
                    ins.then_inc(dense_done, 1)
                if b.ok():
                    pe.wait_ge(av_half_read, b.n * 2 + 1)
                    attend(b, 2)

            run_steps(pe, step)

            pe.wait_ge(seen_ready, B)
            pe.matmul(bank[7][:, 0:E], ones_bf[:, :], seen[:, :], start=True, stop=True).then_inc(counts_done, 1)
            pe.wait_ge(tables_ready, 1)
            pe.wait_ge(experts_loaded, 16 * 2 * E)

            def up_in(r, s, rnd):
                pe.wait_ge(rows_fetched[r], rnd * 16 + 16)
                if not (isinstance(s, int) and s == 0):
                    pe.wait_ge(gx_ready, s)
                for ch in range(DC):
                    ins = pe.transpose(bank[3][:, ch * P:(ch + 1) * P], g_rows[:, r, ch * P:(ch + 1) * P], ident)
                ins.then_inc(gx_transposed, 1)

            def expert(s):
                return pe.value_load(slot_expert[0:1, bass.ds(s, 1)], min_val=0, max_val=E - 1)

            def up(r, s):
                ex = expert(s)
                pe.wait_ge(gx_ready, s + 1)
                pe.matmul(hid_bank[r][:, :], select_bf[:, bass.ds(ex, 1), :].rearrange("p e s -> p (e s)"),
                          bias_parts[:, 0:F], start=True, stop=False)
                for ch in range(DC):
                    ins = pe.matmul(hid_bank[r][:, :], g_xt[:, r, ch, :],
                                    W1[:, bass.ds(ex, 1), ch, :].rearrange("p e n -> p (e n)"),
                                    start=False, stop=(ch == DC - 1))
                ins.then_inc(hid_done, 1)

            def down_in(r, s):
                pe.wait_ge(hid_ready, s + 1)
                if not (isinstance(s, int) and s == 0):
                    pe.wait_ge(hid_t_ready, s)
                for ch in range(FC):
                    ins = pe.transpose(bank[4][:, ch * P:(ch + 1) * P], hid[:, r, ch * P:(ch + 1) * P], ident)
                ins.then_inc(hid_transposed, 1)

            def down(r, s):
                ex = expert(s)
                pe.wait_ge(hid_t_ready, s + 1)
                if not (isinstance(s, int) and s == 0):
                    pe.wait_ge(out_ready, s)
                pe.matmul(bank[5][:, 0:D], select_bf[:, bass.ds(ex, 1), :].rearrange("p e s -> p (e s)"),
                          bias_parts[:, F:F + D], start=True, stop=False)
                for ch in range(FC):
                    ins = pe.matmul(bank[5][:, 0:D], hid_t[:, r, ch, :],
                                    W2[:, bass.ds(ex, 1), ch, :].rearrange("p e n -> p (e n)"),
                                    start=False, stop=(ch == FC - 1))
                ins.then_inc(y_done, 1)

            def slot(k, s, rnd, left=R):
                down_in(k, s)
                if left > 2:
                    up_in((k + 2) % R, s + 2, rnd + (k + 2) // R)
                if left > 1:
                    up((k + 1) % R, s + 1)
                down(k, s)

            up_in(0, 0, 0)
            up_in(1, 1, 0)
            up(0, 0)
            for k in range(R):
                slot(k, k, 0)
            with pe.Fori(1, SLOTS // R - 1) as i:
                for k in range(R):
                    slot(k, i * R + k, i)
            for k in range(R):
                slot(k, SLOTS - R + k, SLOTS // R - 1, left=R - k)


def kernel(x, ctx_1024, g_xattn, g_ffn, L0_xattn_wq_w, L0_xattn_wq_b, L0_xattn_wk_w, L0_xattn_wk_b,
           L0_xattn_wv_w, L0_xattn_wv_b, L0_xattn_dense_w, L0_xattn_dense_b, L0_ffn_router_w,
           L0_ffn_w1, L0_ffn_b1, L0_ffn_w2, L0_ffn_b2):
    import concourse.bacc as bacc
    from concourse.bass_utils import run_bass_kernel_spmd

    def in_chunks(w):
        return np.asarray(w).reshape(-1, P, w.shape[-1]).transpose(1, 0, 2)

    def column(v):
        return np.asarray(v).reshape(-1, P).T

    arrays = {
        "x": x,
        "ctxt": np.asarray(ctx_1024).reshape(B, P, DC, P).transpose(3, 0, 2, 1).reshape(P, B, DC * P),
        "gates": np.concatenate([np.asarray(g_xattn), np.asarray(g_ffn)]).reshape(1, 2),
        "wq": in_chunks(np.asarray(L0_xattn_wq_w).T),
        "wk": in_chunks(np.asarray(L0_xattn_wk_w).T),
        "wv": in_chunks(np.asarray(L0_xattn_wv_w).T),
        "wd": in_chunks(np.asarray(L0_xattn_dense_w).T),
        "bqk": np.concatenate([column(L0_xattn_wq_b), column(L0_xattn_wk_b)], axis=1),
        "bv": column(L0_xattn_wv_b),
        "bd": np.asarray(L0_xattn_dense_b).reshape(1, D),
        "rw": in_chunks(L0_ffn_router_w),
        "w1": np.asarray(L0_ffn_w1).reshape(E, DC, P, F).transpose(0, 2, 1, 3).reshape(E, P, DC * F),
        "w2": np.asarray(L0_ffn_w2).reshape(E, FC, P, D).transpose(0, 2, 1, 3).reshape(E, P, FC * D),
        "b12": np.concatenate([np.asarray(L0_ffn_b1), np.asarray(L0_ffn_b2)], axis=1),
        "consts": build_constants(),
    }
    arrays = {name: np.ascontiguousarray(a) for name, a in arrays.items()}
    nc = bacc.Bacc("TRN2", target_bir_lowering=False, num_devices=1)
    aps = [nc.dram_tensor(name, a.shape, mybir.dt.from_np(a.dtype), kind="ExternalInput").ap()
           for name, a in arrays.items()]
    out = nc.dram_tensor("out", (B, P, D), F32, kind="ExternalOutput").ap()
    flamingo_kernel(nc, *aps, out)
    r = run_bass_kernel_spmd(nc, [arrays], core_ids=[0])
    return r.results[0]["out"]
```
